# Optimizing a Trainium2 kernel written in Bass

```python
import numpy as np
import jax
import jax.numpy as jnp

def _softmax(x, axis=-1):
    return jax.nn.softmax(x, axis=axis)
def _gelu(x):
    return jax.nn.gelu(x, approximate=True)
def _silu(x):
    return jax.nn.silu(x)
def _sigmoid(x):
    return jax.nn.sigmoid(x)
def _layernorm(x, axis=-1, eps=1e-5):
    m = jnp.mean(x, axis=axis, keepdims=True)
    v = jnp.var(x, axis=axis, keepdims=True)
    return (x - m) / jnp.sqrt(v + eps)
def _scatter_add(tgt, idx, src, axis=0):
    return tgt.at[idx].add(src)
def _segment_sum(src, seg, n):
    return jax.ops.segment_sum(src, seg, n)

kernel_name = 'mk_adj_preln_d4_adj_256_03462d'

def setup_inputs(seed: int = 0):
    np.random.seed(seed)
    _w = jnp.asarray
    def _rec_inputs():
        import jax
        import jax.numpy as jnp
        _gk = jax.random.key(seed)
        x = -0.0005146 + 1 * jax.random.normal(jax.random.fold_in(_gk, 1), (8, 2048, 256), jnp.float32)
        _a = jax.random.bernoulli(jax.random.fold_in(_gk, 2), 0.015625, (8, 2048, 2048))
        _a = jnp.logical_or(_a, jnp.swapaxes(_a, -1, -2))
        _a = jnp.logical_or(_a, jnp.eye(2048, dtype=bool))
        adj = _a.astype(jnp.int32)
        return x, adj
    x, adj = _rec_inputs()
    def _L0_gnn_setup():
        import jax, jax.numpy as jnp
        import numpy as np
        B, N, C, OUT, S = (4, 2048, 256, 256, 25)
        DENSITY = 0.008
        key = jax.random.key(seed)
        kA, kX, kW = jax.random.split(key, 3)
        A = jax.random.bernoulli(kA, DENSITY, (B, N, N)).astype(jnp.int32)
        X = jax.random.normal(kX, (B, N, C), dtype=jnp.float32)
        W = jax.random.normal(kW, (2 * C, OUT), dtype=jnp.float32) * np.float32(1.0 / np.sqrt(2 * C))
        b = jnp.zeros((OUT,), dtype=jnp.float32)
        return {'A': A, 'X': X, 'W': W, 'b': b}
    _L0_gnn_all = _L0_gnn_setup()
    _L0_gnn_in = {k: v for k, v in _L0_gnn_all.items() if k in ('W', 'b', )}
    del _L0_gnn_all

    def _L1_gnn_setup():
        import jax, jax.numpy as jnp
        import numpy as np
        NEG_INF = -1000000000.0
        LRELU_ALPHA = 0.2
        key = jax.random.key(seed)
        k1, k2, k3, k4, k5 = jax.random.split(key, 5)
        B, N, Din, H, F = (8, 1024, 256, 4, 64)
        X = jax.random.normal(k1, (B, N, Din), dtype=jnp.float32)
        A = jax.random.randint(k2, (B, N, N), 0, 2).astype(jnp.int32)
        W = jax.random.normal(k3, (Din, H * F), dtype=jnp.float32) * np.sqrt(2.0 / (Din + H * F))
        a_src = jax.random.normal(k4, (H, F), dtype=jnp.float32) * np.sqrt(2.0 / (1 + F))
        a_dst = jax.random.normal(k5, (H, F), dtype=jnp.float32) * np.sqrt(2.0 / (1 + F))
        return {'X': X, 'A': A, 'W': W, 'a_src': a_src, 'a_dst': a_dst}
    _L1_gnn_all = _L1_gnn_setup()
    _L1_gnn_in = {k: v for k, v in _L1_gnn_all.items() if k in ('W', 'a_src', 'a_dst', )}
    del _L1_gnn_all

    def _L2_gnn_setup():
        import jax, jax.numpy as jnp
        import numpy as np
        key = jax.random.key(seed)
        k1, k2, k3, k4 = jax.random.split(key, 4)
        B, N, F, U = (8, 2048, 256, 256)
        x = jax.random.normal(k1, (B, N, F), dtype=jnp.float32)
        adj = jax.random.randint(k2, (B, N, N), 0, 2, dtype=jnp.int32)
        W_msg = jax.random.normal(k3, (F, U), dtype=jnp.float32) / np.sqrt(F)
        W_upd = jax.random.normal(k4, (F, U), dtype=jnp.float32) / np.sqrt(F)
        bias = jnp.zeros((U,), dtype=jnp.float32)
        return {'x': x, 'adj': adj, 'W_msg': W_msg, 'W_upd': W_upd, 'bias': bias}
    _L2_gnn_all = _L2_gnn_setup()
    _L2_gnn_in = {k: v for k, v in _L2_gnn_all.items() if k in ('W_msg', 'W_upd', 'bias', )}
    del _L2_gnn_all

    def _L3_gnn_setup():
        import jax, jax.numpy as jnp
        import numpy as np
        NEG_INF = -1000000000.0
        LEAKY_SLOPE = 0.2
        key = jax.random.key(seed)
        k1, k2, k3, k4 = jax.random.split(key, 4)
        B, N, D_in, D_out = (8, 2048, 256, 256)
        x = jax.random.normal(k1, (B, N, D_in), dtype=jnp.float32)
        adj_matrix = jax.random.randint(k2, (B, N, N), 0, 2, dtype=jnp.int32)
        W = jax.random.normal(k3, (D_out, D_in), dtype=jnp.float32) / np.sqrt(D_in)
        a = jax.random.normal(k4, (1, 2 * D_out), dtype=jnp.float32) / np.sqrt(2 * D_out)
        return {'x': x, 'adj_matrix': adj_matrix, 'W': W, 'a': a}
    _L3_gnn_all = _L3_gnn_setup()
    _L3_gnn_in = {k: v for k, v in _L3_gnn_all.items() if k in ('W', 'a', )}
    del _L3_gnn_all

    return {
        "x": x,
        "adj": adj,
        "L0_gnn_W": _L0_gnn_in["W"],
        "L0_gnn_b": _L0_gnn_in["b"],
        "L1_gnn_W": _L1_gnn_in["W"],
        "L1_gnn_a_src": _L1_gnn_in["a_src"],
        "L1_gnn_a_dst": _L1_gnn_in["a_dst"],
        "L2_gnn_W_msg": _L2_gnn_in["W_msg"],
        "L2_gnn_W_upd": _L2_gnn_in["W_upd"],
        "L2_gnn_bias": _L2_gnn_in["bias"],
        "L3_gnn_W": _L3_gnn_in["W"],
        "L3_gnn_a": _L3_gnn_in["a"],
    }

def reference(x, adj, L0_gnn_W, L0_gnn_b, L1_gnn_W, L1_gnn_a_src, L1_gnn_a_dst, L2_gnn_W_msg, L2_gnn_W_upd, L2_gnn_bias, L3_gnn_W, L3_gnn_a):
    import jax
    import jax.numpy as jnp
    def _L0_gnn_ref(A, X, W, b):
        import jax, jax.numpy as jnp
        import numpy as np
        B, N, C, OUT, S = (4, 2048, 256, 256, 25)
        DENSITY = 0.008
        mask = A != 0
        neg_inf = jnp.float32(-jnp.inf)
        pri = -jnp.arange(N, dtype=jnp.float32)
        scores = jnp.where(mask, pri, neg_inf)
        vals, idx = jax.lax.top_k(scores, S)
        valid = vals > neg_inf
        feats = jax.vmap(lambda x, i: x[i])(X, idx)
        feats = jnp.where(valid[..., None], feats, neg_inf)
        agg = feats.max(axis=2)
        degree = mask.sum(axis=-1)
        agg = jnp.where((degree <= S)[..., None], jnp.maximum(agg, 0.0), agg)
        h = jnp.concatenate([X, agg], axis=-1)
        out = jax.nn.relu(jnp.einsum('bnf,fo->bno', h, W) + b)
        return out

    def _L1_gnn_ref(X, A, W, a_src, a_dst):
        import jax, jax.numpy as jnp
        import numpy as np
        NEG_INF = -1000000000.0
        LRELU_ALPHA = 0.2
        B, N, _ = X.shape
        H, F = a_src.shape
        Wh = (X @ W).reshape(B, N, H, F)
        e_src = jnp.einsum('bnhf,hf->bnh', Wh, a_src)
        e_dst = jnp.einsum('bjhf,hf->bjh', Wh, a_dst)
        e = jax.nn.leaky_relu(e_src[:, :, None, :] + e_dst[:, None, :, :], LRELU_ALPHA)
        mask = (A > 0)[..., None]
        e = jnp.where(mask, e, NEG_INF)
        alpha = jax.nn.softmax(e, axis=2)
        Hout = jnp.einsum('bijh,bjhf->bihf', alpha, Wh)
        Hout = jax.nn.elu(Hout)
        return Hout.reshape(B, N, H * F)

    def _L2_gnn_ref(x, adj, W_msg, W_upd, bias):
        import jax, jax.numpy as jnp
        import numpy as np
        a = adj.astype(x.dtype)
        h = jnp.einsum('bnf,fu->bnu', x, W_msg)
        msg_sum = jnp.einsum('bij,biu->bju', a, h)
        deg = jnp.sum(a, axis=1)
        messages = jnp.where(deg[..., None] > 0, msg_sum / jnp.maximum(deg, 1.0)[..., None], 0.0)
        out = jnp.einsum('bnf,fu->bnu', x, W_upd) + messages + bias
        return jax.nn.relu(out)

    def _L3_gnn_ref(x, adj_matrix, W, a):
        import jax, jax.numpy as jnp
        import numpy as np
        NEG_INF = -1000000000.0
        LEAKY_SLOPE = 0.2
        h = jnp.einsum('bnd,od->bno', x, W)
        D = h.shape[-1]
        a_left, a_right = (a[0, :D], a[0, D:])
        e = (h @ a_left)[:, :, None] + (h @ a_right)[:, None, :]
        e = jnp.where(e > 0, e, LEAKY_SLOPE * e)
        e = jnp.where(adj_matrix == 0, NEG_INF, e)
        alpha = jax.nn.softmax(e, axis=-1)
        return jnp.einsum('bij,bjd->bid', alpha, h)

    h = jnp.maximum(_layernorm(x, axis=-1), 0.0)
    x = x + _L0_gnn_ref(adj, h, L0_gnn_W, L0_gnn_b)
    h = jnp.maximum(_layernorm(x, axis=-1), 0.0)
    x = x + _L1_gnn_ref(h, adj, L1_gnn_W, L1_gnn_a_src, L1_gnn_a_dst)
    h = jnp.maximum(_layernorm(x, axis=-1), 0.0)
    x = x + _L2_gnn_ref(h, adj, L2_gnn_W_msg, L2_gnn_W_upd, L2_gnn_bias)
    h = jnp.maximum(_layernorm(x, axis=-1), 0.0)
    x = x + _L3_gnn_ref(h, adj, L3_gnn_W, L3_gnn_a)
    return x


_drawn_inputs = setup_inputs


def setup_inputs(seed=0):
    import zlib

    import numpy as np

    out = dict(_drawn_inputs(seed))
    spreads = {'L0_gnn_b': (0.0, 0.1), 'L2_gnn_bias': (0.0, 0.1)}
    factors = {'L1_gnn_a_src': 8.0, 'L3_gnn_a': 6.937}
    for name, (base, spread) in spreads.items():
        noise = np.random.default_rng([zlib.crc32(name.encode()), seed]).standard_normal(out[name].shape)
        drawn = base * np.exp(spread * noise) if base else spread * noise
        out[name] = jnp.asarray(drawn.astype(out[name].dtype))
    for name, factor in factors.items():
        out[name] = (out[name] * factor).astype(out[name].dtype)
    return out
```

```python
from contextlib import ExitStack

import concourse.bass as bass
from concourse import mybir

F32 = mybir.dt.float32
BF16 = mybir.dt.bfloat16
I32 = mybir.dt.int32
U32 = mybir.dt.uint32
U8 = mybir.dt.uint8
ALU = mybir.AluOpType
ACT = mybir.ActivationFunctionType
AX = mybir.AxisListType.X

P = 128
B = 8
N = 2048
C = 256
NT = N // P
BLK = 4
NQ = NT // BLK
S = 25
HEADS = 4
F = C // HEADS
WORD = 8
NW = N // WORD
WPT = P // WORD
TAB = N + 1
SLOTS = NT
LAG = 2
EPS = 1e-5
SLOPE = 0.2
LIM = 90.0

C_ID, C_BASE, C_OFF = 0, P, P + NW
C_PACK = C_OFF + B * NT
C_R = C_PACK + WPT
C_BIT = C_R + WORD
C_ONE = C_BIT + WORD
C_END = C_ONE + 1


def constants():
    import numpy as np
    c = np.zeros((P, C_END), np.float32)
    p = np.arange(P)
    c[:, C_ID:C_ID + P] = np.eye(P)
    c[:, C_ONE] = 1.0
    c[:, C_BASE:C_BASE + NW] = (NW - np.arange(NW)) * 256.0
    c[:, C_OFF:C_OFF + B * NT] = N + TAB * (np.arange(B * NT) // NT % 2)
    c[p, C_PACK + p // WORD] = 2.0 ** (WORD - 1 - p % WORD)
    c[:, C_R:C_R + WORD] = np.arange(WORD)
    c[:, C_BIT:C_BIT + WORD] = 2.0 ** (WORD - 1 - np.arange(WORD))
    return c


class Count:

    def __init__(self, sem, credit=0):
        self.sem, self.credit = sem, credit

    def ready(self, n):
        return n + (self.credit + 1)

    def free(self, n, depth):
        assert self.credit >= depth
        return n + (self.credit + 1 - depth)


def gnn_kernel(nc, x, adj, w0, b0, w1, a1s, a1d, w2m, w2u, b2, w3, a3, const, out):
    ctx = ExitStack()
    with ctx:
        def sb(name, shape, dt):
            return ctx.enter_context(nc.sbuf_tensor(name, shape, dt))

        def sem(name):
            return ctx.enter_context(nc.semaphore(name))

        def count(name, credit=0):
            return Count(sem(name), credit)

        htab = nc.dram_tensor("htab", [2 * TAB, C], F32, kind="Internal").ap()
        x1d = nc.dram_tensor("x1d", [B * N, C], F32, kind="Internal").ap()
        u2d = nc.dram_tensor("u2d", [N, C], F32, kind="Internal").ap()
        rows = lambda t: t.rearrange("(t p) c -> p t c", p=P)
        x_r, x1_r, u2_r = rows(x.rearrange("b n c -> (b n) c")), rows(x1d), rows(u2d)
        out_r = rows(out.rearrange("b n c -> (b n) c"))
        adj_r = adj.rearrange("b (i p) j -> p (b i) j", p=P)

        cst = sb("cst", [P, C_END], F32)
        ident, one = cst[:, C_ID:C_ID + P], cst[:, C_ONE:C_ONE + 1]
        ident_bf = sb("ident_bf", [P, P], BF16)
        pack_bf = sb("pack_bf", [P, WPT], BF16)
        bit_u = sb("bit_u", [P, WORD], U32)
        w0_s = sb("w0_s", [P, 4, C], F32)
        w1_s = sb("w1_s", [P, 2, C + 2 * HEADS], F32)
        w2_s = sb("w2_s", [P, 2, 2 * C], F32)
        w3_s = sb("w3_s", [P, 2, C + 2], F32)
        bias = sb("bias", [P // 4 + 1, C], F32)
        adj_i = sb("adj_i", [P, 2, 512], I32)
        adj_b = sb("adj_b", [P, 2, 512], BF16)
        adjT_b = sb("adjT_b", [P, 1024], BF16)
        adjT = sb("adjT", [P, NT, 2 * N], U8)
        key = sb("key", [P, NW], F32)
        top = sb("top", [P, 32], F32)
        topu = sb("topu", [P, S], U32)
        hi8 = sb("hi8", [P, S], U32)
        bits = sb("bits", [P, S, WORD], U32)
        score = key[:, 0:S * WORD].rearrange("p (s r) -> p s r", s=S)
        idx = sb("idx", [P, 2, S], U32)
        gath = sb("gath", [P, 2, S, C], F32)
        cat = sb("cat", [P, 2 * C], F32)
        catT = sb("catT", [P, 4, P], F32)
        x1 = sb("x1", [P, C], F32)
        xa = sb("xa", [P, 2, C], F32)
        st_a = sb("st_a", [P, 2, 6], F32)
        mv_a = sb("mv_a", [P, 2, 2], F32)
        rn_a = sb("rn_a", [P, 2, 2], F32)
        xr = sb("xr", [P, NT, C], F32)
        hb = sb("hb", [P, BLK, C], F32)
        st = sb("st", [P, NT, 6], F32)
        mv = sb("mv", [P, NT, 2], F32)
        rs = sb("rs", [P, NT], F32)
        nm = sb("nm", [P, NT], F32)
        tmp = sb("tmp", [P, NT], F32)
        tmp_a = sb("tmp_a", [P, 2], F32)
        sd = sb("sd", [P, NT, 2 * HEADS], F32)
        dmx = sb("dmx", [P, HEADS], F32)
        dtop = sb("dtop", [HEADS, 1], F32)
        ddiag = sb("ddiag", [HEADS, HEADS], F32)
        dd = sb("dd", [P, NT, HEADS], F32)
        sp_ = sb("sp_", [P, NT, HEADS], F32)
        vv = sb("vv", [P, NT, HEADS], F32)
        gg = sb("gg", [P, NT, HEADS], F32)
        sq = sb("sq", [P, BLK, HEADS], F32)
        den = sb("den", [P, BLK, HEADS], F32)
        col_i = sb("col_i", [P, 2, 4, P], I32)
        col_b = sb("col_b", [P, 2, 4, P], BF16)
        val_cols = NT * HEADS * (F + 1)
        region = sb("region", [P, val_cols + HEADS * 512], F32)
        V = {1: region[:, 0:val_cols].rearrange("p (t c) -> p t c", t=NT),
             3: region[:, 0:NT * (C + 1)].rearrange("p (t c) -> p t c", t=NT)}
        wB = region[:, val_cols:val_cols + HEADS * 512].rearrange("p (h i) -> p h i", h=HEADS)
        y_s = region[:, val_cols:val_cols + BLK * C].rearrange("p (t c) -> p t c", t=BLK)
        e_s = region[:, val_cols + BLK * C:val_cols + 2 * BLK * C].rearrange("p (t c) -> p t c", t=BLK)
        SPL = 3 * C + 2
        split = region[:, 0:NT * SPL // 2].bitcast(BF16).rearrange("p (t c) -> p t c", t=NT)
        edge = sb("edge", [P, 4, 512], F32)
        edge_f = edge[:, :, :].rearrange("p a c -> p (a c)")
        hT = edge_f[:, 0:1024].rearrange("p (t k r) -> p t k r", t=BLK, k=2)
        res = edge_f[:, 1024:2048].rearrange("p (t c) -> p t c", t=BLK)
        u2_s = edge_f[:, 0:1024].rearrange("p (t c) -> p t c", t=BLK)

        def pb(name, shape, dt):
            return ctx.enter_context(nc.psum_tensor(name, shape, dt))

        acc = pb("acc", [P, BLK, 512], F32)
        psT = pb("psT", [P, 1024], BF16)
        psH = pb("psH", [P, 512], F32)
        psO = pb("psO", [P, 512], F32)
        psB = pb("psB", [P, 512], F32)
        o_mm, words = psO[:, 0:C], psO[:, C:2 * C]

        w_ld, w_cast, w_red, w_tr, w_ev, w_done = (sem(n) for n in ("w_ld", "w_cast", "w_red", "w_tr", "w_ev", "w_done"))
        tiles_begun, loads_begun = sem("tiles_begun"), sem("loads_begun")
        zero_st, zero_set = sem("zero_st"), sem("zero_set")
        chain = sem("chain")
        a_ld = [sem("a_ld0"), sem("a_ld1")]
        a_cast, a_used = count("a_cast", 2), count("a_used", 2)
        a_evac, a_pack = count("a_evac", 1), count("a_pack", 1)
        a_key, idx_ready, reduced = count("a_key", 1), count("idx_ready"), count("reduced", 2)
        gathered = [sem("gathered0"), sem("gathered1")]
        xa_ld = [sem("xa_ld0"), sem("xa_ld1")]
        a_ln, a_relu = count("a_ln"), count("a_relu", 2)
        h_dma, h_stored = sem("h_dma"), count("h_stored")
        cat_ld, x1_ld = sem("cat_ld"), sem("x1_ld")
        cat_tr, cat_ev, o_done, x1_done = (count(n, m) for n, m in (("cat_tr", 1), ("cat_ev", 1), ("o_done", 1), ("x1_done", 3)))
        x1_dma, x1_stored = sem("x1_dma"), count("x1_stored")
        xr_ld = sem("xr_ld")
        ln_ok = {p: count(f"ln{p}") for p in (1, 2, 3)}
        h_ok = {p: count(f"h{p}", 1) for p in (1, 2, 3)}
        tp_ok = {p: count(f"tp{p}", 1) for p in (1, 2, 3)}
        hT_ok = {p: count(f"hT{p}") for p in (1, 2, 3)}
        dn_ok = {p: count(f"dn{p}", 1) for p in (1, 2, 3)}
        ev_ok = {p: count(f"ev{p}", 1) for p in (1, 2, 3)}
        hi_ok, ut_ok, u_dma, u_stored = count("hi_ok"), count("ut_ok", 1), sem("u_dma"), count("u_stored", 1)
        gd = {p: sem(f"gd{p}") for p in (1, 3)}
        gp = {p: sem(f"gp{p}") for p in (1, 3)}
        ga = {p: sem(f"ga{p}") for p in (1, 3)}
        sq_ok = {p: count(f"sq{p}") for p in (1, 3)}
        sB_ok = {p: count(f"sB{p}") for p in (1, 3)}
        wB_ok = {p: count(f"wB{p}", 1) for p in (1, 3)}
        edge_ok = {p: count(f"edge{p}") for p in (1, 3)}
        mm_ok = {p: count(f"mm{p}", 4) for p in (1, 3)}
        x_ok = {p: count(f"x{p}", 1) for p in (1, 3)}
        y_ok, e_ok = count("y_ok"), count("e_ok")
        out_st = sem("out_st")
        c_ld = [sem("c_ld0"), sem("c_ld1")]
        c_cast, c_mm, x2_ok, u_ld = count("c_cast", 2), count("c_mm", 2), count("x2_ok", 4), sem("u_ld")

        def front_tile(b, sh, par):
            return 16 * (b + 1) + LAG + 2 * sh + par

        def back_tile(b, sh, par):
            return 16 * (b + 1) + 2 * sh + par

        def half(b, sh):
            return 8 * (b + 1) + sh

        def body(eng, b, do, front=lambda sh: True, pre=True, slots=True, unroll_last=False):
            def slot(sh, par, part, with_pre=False):
                if slots:
                    do.slot(b, sh, par, part, front(sh), with_pre and pre)

            do.fetch(b)
            do.norm(1, b)
            for g in loop(eng, NQ):
                do.prep(1, b, g)
            do.spread(1, b)
            with eng.Fori(0, NQ) as q:
                slot(q, 0, 1, True)
                do.attend_start(1, b, q)
                do.attend(1, b, q, 0, 4)
                slot(q, 0, 2, True)
                do.attend(1, b, q, 4, 8)
                slot(q, 0, 3, True)
                slot(q, 1, 1, True)
                do.attend(1, b, q, 8, 12)
                slot(q, 1, 2, True)
                do.attend(1, b, q, 12, 16)
                slot(q, 1, 3, True)
                do.attend_end(1, b, q)
            do.norm(2, b)
            for g in loop(eng, NQ):
                do.prep(2, b, g)
            with eng.Fori(0, NQ // 2) as r:
                for par in range(2):
                    q = 2 * r + par
                    do.mean_start(b, q)
                    slot(4 + r, par, 1)
                    do.mean(b, q, 0)
                    slot(4 + r, par, 2)
                    do.mean(b, q, 1)
                    do.mean(b, q, 2)
                    slot(4 + r, par, 3)
                    do.mean(b, q, 3)
            do.norm(3, b)
            for g in loop(eng, NQ):
                do.prep(3, b, g)
            do.spread(3, b)

            def last(r, sh):
                for par in range(2):
                    q = 2 * r + par
                    slot(sh, par, 1)
                    do.attend_start(3, b, q)
                    do.attend(3, b, q, 0, 5)
                    slot(sh, par, 2)
                    do.attend(3, b, q, 5, 11)
                    slot(sh, par, 3)
                    do.attend(3, b, q, 11, 16)
                    do.attend_end(3, b, q)

            if unroll_last:
                for r in range(NQ // 2):
                    last(r, 6 + r)
            else:
                with eng.Fori(0, NQ // 2) as r:
                    last(r, 6 + r)
            do.end(b)

        def loop(eng, n):
            with eng.Fori(0, n) as i:
                yield i

        def program(eng, do):
            do.setup()
            with eng.Fori(0, NT // 2) as i:
                for part in (1, 3):
                    do.pre(2 * i, i, part)
            for T in range(LAG):
                for part in (1, 2, 3):
                    do.slot_front(T, T, 0, part)
            for first in (0, 4):
                with eng.Fori(first, first + 4) as sh:
                    for par in range(2):
                        for part in (1, 2, 3):
                            do.slot(-1, sh, par, part, True, first == 0)
            with eng.Fori(0, B - 2) as b:
                body(eng, b, do)
            body(eng, B - 2, do, front=lambda sh: not (isinstance(sh, int) and sh == 7), pre=False, unroll_last=True)
            body(eng, B - 1, do, slots=False)

        class Part:
            def setup(self): pass
            def pre(self, u, n, part): pass
            def slot_front(self, T, par, n, part): pass
            def slot_back(self, T, par, n, part, front): pass
            def prep(self, p, b, g): pass
            def spread(self, p, b): pass
            def attend_start(self, p, b, q): pass
            def attend(self, p, b, q, j0, j1): pass
            def attend_end(self, p, b, q): pass
            def fetch(self, b): pass
            def norm(self, p, b): pass
            def mean_start(self, b, q): pass
            def mean(self, b, q, k): pass
            def end(self, b): pass

            def slot(self, b, sh, par, part, front, with_pre):
                Tb, n = back_tile(b, sh, par), half(b, sh)
                if part == 1:
                    self.slot_back(Tb, par, n, 1, front)
                    if with_pre:
                        self.pre(16 * (b + 2) + 4 * sh + 2 * par, 8 * (b + 2) + 2 * sh + par, 1)
                    if front:
                        self.slot_front(front_tile(b, sh, par), par, n + LAG // 2, 1)
                else:
                    if front:
                        self.slot_front(front_tile(b, sh, par), par, n + LAG // 2, part)
                    if with_pre and part == 3:
                        self.pre(16 * (b + 2) + 4 * sh + 2 * par, 8 * (b + 2) + 2 * sh + par, 3)
                    self.slot_back(Tb, par, n, part, front)

        def table_row(T):
            return (T % (2 * NT)) * P + (T % (2 * NT)) // NT

        def heads(p):
            return HEADS if p == 1 else 1

        block = ctx.enter_context(nc.Block())

        @block.sync
        def _(sp):
            class Do(Part):
                def setup(self):
                    sp.sem_inc(u_stored.sem, u_stored.credit)
                    kp = "(k p) n -> p k n"
                    tmp = gath[:, 0, :, :]
                    loads = [
                        (cst[:, :], const), (w0_s[:, :, :], w0.rearrange(kp, p=P)),
                        (w1_s[:, :, 0:C], w1.rearrange(kp, p=P)),
                        (w2_s[:, :, 0:C], w2m.rearrange(kp, p=P)), (w2_s[:, :, C:2 * C], w2u.rearrange(kp, p=P)),
                        (tmp[:, 0:2, :], w3.rearrange(kp, p=P)),
                        (tmp[:, 2, :], a1s.rearrange("h f -> (h f)").partition_broadcast(P)),
                        (tmp[:, 3, :], a1d.rearrange("h f -> (h f)").partition_broadcast(P)),
                        (tmp[:, 4:6, :], a3.rearrange("a (k c) -> (a k) c", k=2).partition_broadcast(P)),
                        (bias[0:1, :], b0.rearrange("(a c) -> a c", a=1)),
                        (bias[32:33, :], b2.rearrange("(a c) -> a c", a=1)),
                    ]
                    assert len(loads) == N_LOADS
                    for to, fr in loads:
                        sp.dma_start(to, fr).then_inc(w_ld, 16)
                    sp.wait_ge(zero_set, 1)
                    for i in range(2):
                        sp.dma_start(htab[i * N:i * N + N, :].rearrange("(p t) c -> p (t c)", p=P), xr[:, :, :].rearrange("p t c -> p (t c)")).then_inc(zero_st, 16)
                    sp.dma_start(htab[2 * N:2 * TAB, :], xr[0:2, 0, :]).then_inc(zero_st, 16)
                    sp.wait_ge(zero_st, 48)

                def pre(self, u, n, part):
                    for i in range(2):
                        if part == 1:
                            sp.dma_start(xa[:, i, :], x_r[:, bass.ds(u + i, 1), :].rearrange("p t c -> p (t c)")).then_inc(xa_ld[i], 16)
                        else:
                            sp.wait_ge(a_relu.sem, a_relu.ready(u + i))
                            sp.dma_start(htab[bass.ds(table_row(u + i), P), :], xa[:, i, :]).then_inc(h_dma, 16)
                            sp.wait_ge(h_dma, 16 * (u + i) + 16)
                            sp.sem_inc(h_stored.sem, 1)

                def slot_front(self, T, par, n, part):
                    if part != 1:
                        return
                    for k in range(4):
                        sp.wait_ge(a_cast.sem, a_cast.free(4 * T + k, 2))
                        sp.dma_start(adj_i[:, k % 2, :], adj_r[:, bass.ds(T, 1), 512 * k:512 * k + 512].rearrange("p t c -> p (t c)")).then_inc(a_ld[k % 2], 16)

                def slot_back(self, T, par, n, part, front):
                    if part == 1:
                        sp.wait_ge(cat_tr.sem, cat_tr.free(T, 1))
                        sp.dma_start(cat[:, 0:C], htab[bass.ds(table_row(T), P), :]).then_inc(cat_ld, 16)
                        sp.dma_start(x1[:, :], x_r[:, bass.ds(T, 1), :].rearrange("p t c -> p (t c)")).then_inc(x1_ld, 16)
                    if part == 3:
                        sp.wait_ge(x1_done.sem, x1_done.ready(T))
                        sp.dma_start(x1_r[:, bass.ds(T, 1), :].rearrange("p t c -> p (t c)"), x1[:, :]).then_inc(x1_dma, 16)
                        sp.wait_ge(x1_dma, 16 * T + 16)
                        sp.sem_inc(x1_stored.sem, 1)

                def fetch(self, b):
                    for g in range(NQ):
                        sp.dma_start(xr[:, BLK * g:BLK * g + BLK, :], x1_r[:, bass.ds(NT * b + BLK * g, BLK), :]).then_inc(xr_ld, 16)
                        sp.wait_ge(xr_ld, 16 * (NQ * b + g) + 16)
                        sp.sem_inc(loads_begun, 1)

                def prep(self, p, b, g):
                    G = NQ * b + g
                    if p == 2:
                        sp.wait_ge(ut_ok.sem, ut_ok.ready(G))
                        sp.dma_start(u2_r[:, bass.ds(BLK * g, BLK), :], hb[:, :, :]).then_inc(u_dma, 16)
                        sp.wait_ge(u_dma, 16 * G + 16)
                        sp.sem_inc(u_stored.sem, 1)

                def mean_start(self, b, q):
                    Q = NQ * b + q
                    sp.wait_ge(ev_ok[2].sem, ev_ok[2].ready(NQ * b + NQ - 1))
                    sp.wait_ge(x2_ok.sem, x2_ok.free(4 * Q + 3, 4))
                    sp.dma_start(u2_s, u2_r[:, bass.ds(BLK * q, BLK), :]).then_inc(u_ld, 16)

                def mean(self, b, q, k):
                    for m in range(4):
                        n = 4 * (4 * (NQ * b + q) + k) + m
                        sp.wait_ge(c_cast.sem, c_cast.free(n, 2))
                        sp.dma_start(col_i[:, m % 2, :, :], adj_r[:, bass.ds(NT * b + 4 * m, 4), bass.ds((4 * q + k) * P, P)]).then_inc(c_ld[m % 2], 16)

                def attend_end(self, p, b, q):
                    if p == 3:
                        Q = NQ * b + q
                        sp.wait_ge(x_ok[3].sem, x_ok[3].ready(Q))
                        sp.dma_start(out_r[:, bass.ds(BLK * Q, BLK), :], xr[:, bass.ds(BLK * q, BLK), :]).then_inc(out_st, 16)

                def end(self, b):
                    sp.wait_ge(out_st, 16 * NQ * (b + 1))
                    sp.sem_inc(loads_begun, 1)

            program(sp, Do())

        @block.gpsimd
        def _(pool):
            class Do(Part):
                def slot_front(self, T, par, n, part):
                    if part != 2:
                        return
                    pool.wait_ge(h_stored.sem, (T // NT) * NT + NT)
                    pool.wait_ge(reduced.sem, reduced.free(T, 2))
                    pool.wait_ge(idx_ready.sem, idx_ready.ready(T))
                    pool.sem_inc(tiles_begun, 1)
                    for s in range(S):
                        pool.indirect_dma_start(
                            out=gath[:, par, s, :], out_offset=None, in_=htab,
                            in_offset=bass.IndirectOffsetOnAxis(ap=idx[:, par, s:s + 1], axis=0),
                        ).then_inc(gathered[par], 16)

            program(pool, Do())

        @block.scalar
        def _(act):
            class Do(Part):
                def setup(self):
                    for c in (a_cast, a_evac, a_relu, cat_ev, h_ok[1], h_ok[2], h_ok[3], ev_ok[1], ev_ok[3], ut_ok, wB_ok[1], wB_ok[3], c_cast):
                        act.sem_inc(c.sem, c.credit)
                    act.wait_ge(w_ld, 16 * N_LOADS)
                    act.activation(ident_bf[:, :], ident, ACT.Copy).then_inc(w_cast, 1)
                    act.activation(pack_bf[:, :], cst[:, C_PACK:C_PACK + WPT], ACT.Copy).then_inc(w_cast, 1)
                    act.wait_ge(w_tr, 1)
                    act.activation(w3_s[:, :, 0:C], psH[:, :].rearrange("p (k o) -> p k o", k=2), ACT.Copy).then_inc(w_ev, 1)

                def pre(self, u, n, part):
                    if part == 3:
                        for i in range(2):
                            act.wait_ge(a_ln.sem, a_ln.ready(u + i))
                            act.activation(xa[:, i, :], xa[:, i, :], ACT.Relu, bias=rn_a[:, i, 1:2], scale=rn_a[:, i, 0:1]).then_inc(a_relu.sem, 1)

                def slot_front(self, T, par, n, part):
                    if part != 1:
                        return

                    def cast(k):
                        act.wait_ge(a_ld[k % 2], 32 * T + 16 * (k // 2) + 16)
                        act.wait_ge(a_used.sem, a_used.free(4 * T + k, 2))
                        act.activation(adj_b[:, k % 2, :], adj_i[:, k % 2, :], ACT.Copy).then_inc(a_cast.sem, 1)

                    for half in range(2):
                        for k in range(2):
                            cast(2 * half + k)
                        act.wait_ge(a_used.sem, a_used.ready(4 * T + 2 * half + 1))
                        act.wait_ge(a_pack.sem, a_pack.free(2 * T + half, 1))
                        act.activation(adjT_b[:, :], psT[:, :], ACT.Copy)
                        act.activation(adjT[:, 8 * half:8 * half + 8, bass.ds((T % (2 * NT)) * P, P)],
                                       psT[:, :].rearrange("p (j i) -> p j i", j=8), ACT.Copy).then_inc(a_evac.sem, 1)

                def slot_back(self, T, par, n, part, front):
                    if part == 2:
                        act.wait_ge(cat_tr.sem, cat_tr.ready(T))
                        act.wait_ge(o_done.sem, o_done.free(T, 1))
                        act.activation(catT[:, :, :].rearrange("p k r -> p (k r)"), psH[:, :], ACT.Copy).then_inc(cat_ev.sem, 1)

                def prep(self, p, b, g):
                    G = NQ * b + g
                    act.wait_ge(ln_ok[p].sem, ln_ok[p].ready(b))
                    act.wait_ge(tp_ok[p].sem, tp_ok[p].free(G, 1))
                    if p == 2:
                        act.wait_ge(u_stored.sem, u_stored.free(G, 1))
                    for k in range(BLK):
                        ins = act.activation(hb[:, k, :], xr[:, bass.ds(BLK * g + k, 1), :].rearrange("p t c -> p (t c)"),
                                             ACT.Relu, bias=nm[:, bass.ds(BLK * g + k, 1)], scale=rs[:, bass.ds(BLK * g + k, 1)])
                    ins.then_inc(h_ok[p].sem, 1)
                    act.wait_ge(tp_ok[p].sem, tp_ok[p].ready(G))
                    act.wait_ge(dn_ok[p].sem, dn_ok[p].free(G, 1))
                    for k in range(2):
                        ins = act.activation(edge_f[:, 512 * k:512 * k + 512], acc[:, k, :], ACT.Copy)
                    ins.then_inc(hT_ok[p].sem, 1)
                    act.wait_ge(dn_ok[p].sem, dn_ok[p].ready(G))
                    if p == 2:
                        act.activation(split[:, bass.ds(BLK * g, BLK), 2 * C:3 * C], acc[:, :, 0:C], ACT.Copy).then_inc(hi_ok.sem, 1)
                        act.activation(hb[:, :, :], acc[:, :, C:2 * C], ACT.Copy).then_inc(ut_ok.sem, 1)
                        return
                    H = heads(p)
                    D = C // H
                    for k in range(BLK):
                        to = V[p][:, bass.ds(BLK * g + k, 1), :].rearrange("p t (h f) -> p (t h) f", h=H)[:, :, 0:D]
                        act.activation(to, acc[:, k, 0:C].rearrange("p (h f) -> p h f", h=H), ACT.Copy)
                    act.activation(sd[:, bass.ds(BLK * g, BLK), 0:2 * H], acc[:, :, C:C + 2 * H], ACT.Copy).then_inc(ev_ok[p].sem, 1)

                def spread(self, p, b):
                    H = heads(p)
                    act.wait_ge(gd[p], 4 * b + 3)
                    act.activation(vv[:, :, 0:H], dd[:, :, 0:H], ACT.Exp)
                    act.activation(gg[:, :, 0:H], dd[:, :, 0:H], ACT.Exp, scale=-(1 - SLOPE)).then_inc(ga[p], 1)

                def attend_start(self, p, b, q):
                    H, Q = heads(p), NQ * b + q
                    act.wait_ge(x_ok[p].sem, x_ok[p].free(Q, 1))
                    for h in range(H):
                        act.wait_ge(sB_ok[p].sem, sB_ok[p].ready(H * Q + h))
                        act.activation(wB[:, h, :], psB[:, :], ACT.Exp, scale=1 - SLOPE).then_inc(wB_ok[p].sem, 1)

                def attend_end(self, p, b, q):
                    if p == 1:
                        Q = NQ * b + q
                        act.wait_ge(y_ok.sem, y_ok.ready(Q))
                        act.activation(e_s, y_s, ACT.Exp).then_inc(e_ok.sem, 1)

                def mean(self, b, q, k):
                    for m in range(4):
                        J = 4 * (NQ * b + q) + k
                        act.wait_ge(c_ld[m % 2], 32 * J + 16 * (m // 2) + 16)
                        act.wait_ge(c_mm.sem, c_mm.free(4 * J + m, 2))
                        act.activation(col_b[:, m % 2, :, :], col_i[:, m % 2, :, :], ACT.Copy).then_inc(c_cast.sem, 1)

            program(act, Do())

        @block.tensor
        def _(pe):
            class Do(Part):
                def setup(self):
                    for c in (a_used, a_pack, cat_tr, o_done, tp_ok[1], tp_ok[2], tp_ok[3], dn_ok[1], dn_ok[2], dn_ok[3], mm_ok[1], mm_ok[3], c_mm):
                        pe.sem_inc(c.sem, c.credit)
                    pe.wait_ge(w_ld, 16 * N_LOADS)
                    for dk in range(2):
                        for ok in range(2):
                            ins = pe.transpose(psH[:, dk * C + ok * P:dk * C + ok * P + P], gath[:, 0, ok, dk * P:dk * P + P], ident)
                    ins.then_inc(w_tr, 1)
                    pe.wait_ge(w_cast, 2)
                    pe.wait_ge(w_done, 1)

                def slot_front(self, T, par, n, part):
                    if part != 1:
                        return

                    for half in range(2):
                        pe.wait_ge(a_evac.sem, a_evac.free(2 * T + half, 1))
                        for k in range(2):
                            pe.wait_ge(a_cast.sem, a_cast.ready(4 * T + 2 * half + k))
                            for j in range(4):
                                ins = pe.transpose(psT[:, 512 * k + P * j:512 * k + P * j + P], adj_b[:, k, P * j:P * j + P], ident_bf[:, :])
                            ins.then_inc(a_used.sem, 1)
                        pe.wait_ge(a_evac.sem, a_evac.ready(2 * T + half))
                        if half == 0:
                            pe.wait_ge(a_key.sem, a_key.free(T, 1))
                            pe.wait_ge(x1_done.sem, x1_done.ready(T - LAG - 1))
                        for j in range(8):
                            w = WPT * (8 * half + j)
                            ins = pe.matmul(words[:, w:w + WPT], adjT_b[:, P * j:P * j + P], pack_bf[:, :], start=True, stop=True)
                        ins.then_inc(a_pack.sem, 1)

                def slot_back(self, T, par, n, part, front):
                    if part != 2:
                        return
                    pe.wait_ge(cat_ld, 16 * T + 16)
                    pe.wait_ge(reduced.sem, reduced.ready(T))
                    pe.wait_ge(cat_ev.sem, cat_ev.free(T, 1))
                    for k in range(4):
                        ins = pe.transpose(psH[:, P * k:P * k + P], cat[:, P * k:P * k + P], ident)
                    ins.then_inc(cat_tr.sem, 1)
                    pe.wait_ge(x1_done.sem, x1_done.free(T, 1))
                    if front:
                        pe.wait_ge(a_key.sem, a_key.ready(T + LAG))
                    pe.matmul(o_mm, one[0:1, :].to_broadcast([1, P]), bias[0:1, :], start=True, stop=False)
                    pe.wait_ge(cat_ev.sem, cat_ev.ready(T))
                    for k in range(4):
                        ins = pe.matmul(o_mm, catT[:, k, :], w0_s[:, k, :], start=False, stop=(k == 3))
                    ins.then_inc(o_done.sem, 1)

                def prep(self, p, b, g):
                    G = NQ * b + g
                    pe.wait_ge(h_ok[p].sem, h_ok[p].ready(G))
                    pe.wait_ge(ev_ok[p].sem, ev_ok[p].free(G, 1))
                    if p == 2:
                        pe.wait_ge(ut_ok.sem, ut_ok.free(G, 1))
                    for k in range(BLK):
                        for c in range(2):
                            at = (k % 2) * C + c * P
                            ins = pe.transpose(acc[:, k // 2, at:at + P], hb[:, k, c * P:c * P + P], ident)
                    ins.then_inc(tp_ok[p].sem, 1)
                    pe.wait_ge(hT_ok[p].sem, hT_ok[p].ready(G))
                    w = {1: w1_s, 2: w2_s, 3: w3_s}[p]
                    n = w.shape[2]
                    for k in range(BLK):
                        for c in range(2):
                            ins = pe.matmul(acc[:, k, 0:n], hT[:, k, c, :], w[:, c, :], start=(c == 0), stop=(c == 1 and p != 2),
                                            skip_group_check=True)
                        if p == 2:
                            ins = pe.matmul(acc[:, k, C:2 * C], one[32:33, :].to_broadcast([1, P]), bias[32:33, :], start=False, stop=True,
                                            skip_group_check=True)
                    ins.then_inc(dn_ok[p].sem, 1)

                def spread(self, p, b):
                    H = heads(p)
                    pe.wait_ge(gd[p], 4 * b + 1)
                    pe.transpose(psB[0:H, 0:P], dmx[:, 0:H], ident).then_inc(gp[p], 1)
                    pe.wait_ge(gd[p], 4 * b + 2)
                    pe.matmul(psB[:, P:P + H], one[0:H, :].to_broadcast([H, P]), ddiag[0:H, 0:H], start=True, stop=True).then_inc(gp[p], 1)

                def attend_start(self, p, b, q):
                    H, Q = heads(p), NQ * b + q
                    pe.wait_ge(sq_ok[p].sem, sq_ok[p].ready(Q))
                    for h in range(H):
                        pe.wait_ge(wB_ok[p].sem, wB_ok[p].free(H * Q + h, 1))
                        for k in range(BLK):
                            ins = pe.matmul(psB[:, P * k:P * k + P], sq[:, k, h:h + 1].to_broadcast([P, P]), ident, start=True, stop=True)
                        ins.then_inc(sB_ok[p].sem, 1)

                def attend(self, p, b, q, j0, j1):
                    H, Q = heads(p), NQ * b + q
                    D = C // H + 1
                    if j0 == 0:
                        pe.wait_ge(gd[p], 4 * b + 4)
                        pe.wait_ge(x_ok[p].sem, x_ok[p].free(Q, 1))
                    for J in range(j0, j1):
                        for h in range(H):
                            n = H * J + h
                            pe.wait_ge(edge_ok[p].sem, edge_ok[p].ready(NT * H * Q + n))
                            for k in range(BLK):
                                ins = pe.matmul(acc[:, k, D * h:D * h + D], edge[:, n % 4, P * k:P * k + P], V[p][:, J, D * h:D * h + D],
                                                start=(n == 0), stop=(J == NT - 1), skip_group_check=True)
                            ins.then_inc(mm_ok[p].sem, 1)

                def mean(self, b, q, k):
                    J = 4 * (NQ * b + q) + k
                    if k == 0:
                        pe.wait_ge(ev_ok[2].sem, ev_ok[2].ready(NQ * b + NQ - 1))
                    pe.wait_ge(x2_ok.sem, x2_ok.free(J, 4))
                    for m in range(4):
                        pe.wait_ge(c_cast.sem, c_cast.ready(4 * J + m))
                        for i in range(4):
                            t = 4 * m + i
                            w = col_b[:, m % 2, i, :]
                            pe.matmul(acc[:, k, 0:C + 1], w, split[:, t, 2 * C:3 * C + 1], start=(t == 0), stop=False, skip_group_check=True)
                            pe.matmul(acc[:, k, 0:C], w, split[:, t, 0:C], start=False, stop=False, skip_group_check=True)
                            ins = pe.matmul(acc[:, k, 0:C], w, split[:, t, C:2 * C], start=False, stop=(t == NT - 1), skip_group_check=True)
                        ins.then_inc(c_mm.sem, 1)

            program(pe, Do())

        @block.vector
        def _(dve):
            class Steps:
                n = 0

                def of(self, ins):
                    ins.then_inc(chain, 1)
                    self.n += 1

                def wait(self):
                    dve.wait_ge(chain, self.n)

                def carry(self):
                    dve.sem_inc(chain, 1)
                    self.n += 1

                def end(self):
                    self.wait()
                    dve.sem_clear(chain)
                    self.n = 0

            steps = Steps()

            def deviation(mean, var, rstd, shift, tmp):
                steps.of(dve.tensor_scalar(var, var, EPS, None, ALU.add))
                steps.wait()
                steps.of(dve.tensor_scalar(tmp.bitcast(U32), var.bitcast(U32), 1, None, ALU.logical_shift_right))
                steps.wait()
                steps.of(dve.tensor_scalar(rstd.bitcast(U32), tmp.bitcast(U32), -1.0, float(0x5F3759DF), ALU.mult, ALU.add))
                for _ in range(3):
                    steps.wait()
                    steps.of(dve.scalar_tensor_tensor(tmp, rstd, -0.5, rstd, ALU.mult, ALU.mult))
                    steps.wait()
                    steps.of(dve.tensor_tensor(tmp, tmp, var, ALU.mult))
                    steps.wait()
                    steps.of(dve.scalar_tensor_tensor(rstd, tmp, 1.5, rstd, ALU.add, ALU.mult))
                steps.wait()
                return dve.scalar_tensor_tensor(shift, mean, -1.0, rstd, ALU.mult, ALU.mult)

            def block_stats(q):
                for k in range(BLK):
                    steps.of(dve.bn_stats(st[:, bass.ds(BLK * q + k, 1), :].rearrange("p t c -> p (t c)"),
                                          xr[:, bass.ds(BLK * q + k, 1), :].rearrange("p t c -> p (t c)")))

            def first_bits(values, n_rounds):
                for r in range(n_rounds):
                    steps.of(dve.max(top[:, 8 * r:8 * r + 8], values))
                    steps.wait()
                    if r < n_rounds - 1:
                        steps.of(dve.match_replace(values, top[:, 8 * r:8 * r + 8], values, 0.0))
                        steps.wait()

            class Do(Part):
                def setup(self):
                    for c in (a_key, reduced, x1_done, ev_ok[2], x_ok[1], x_ok[3], x2_ok):
                        dve.sem_inc(c.sem, c.credit)
                    dve.memset(xr[:, :, :], 0.0).then_inc(zero_set, 1)
                    dve.wait_ge(w_ld, 16 * N_LOADS)
                    steps.of(dve.tensor_copy(bit_u[:, :], cst[:, C_BIT:C_BIT + WORD]))
                    steps.of(dve.tensor_scalar(bias[0:1, :], bias[0:1, :], -1.0, None, ALU.add))
                    scratch = gath[:, 1, 0, :]
                    dve.wait_ge(w_ev, 1)
                    for w, k, at, a, H in [(w1_s, k, C, 2, HEADS) for k in range(2)] + [(w1_s, k, C + HEADS, 3, HEADS) for k in range(2)] \
                            + [(w3_s, k, C, 4, 1) for k in range(2)] + [(w3_s, k, C + 1, 5, 1) for k in range(2)]:
                        steps.of(dve.tensor_tensor(scratch, w[:, k, 0:C], gath[:, 0, a, :], ALU.mult))
                        steps.wait()
                        steps.of(dve.tensor_reduce(w[:, k, at:at + H], scratch.rearrange("p (h f) -> p h f", h=H), AX, ALU.add))
                        steps.wait()
                    steps.end()
                    dve.sem_inc(w_done, 1)
                    dve.wait_ge(w_done, 1)

                def pre(self, u, n, part):
                    if part != 3:
                        return
                    for i in range(2):
                        dve.wait_ge(xa_ld[i], 16 * n + 16)
                        dve.wait_ge(a_relu.sem, a_relu.free(u + i, 2))
                        steps.of(dve.bn_stats(st_a[:, i, :], xa[:, i, :]))
                    steps.wait()
                    for i in range(2):
                        steps.of(dve.bn_aggr(mv_a[:, i, :], st_a[:, i, :]))
                    steps.wait()
                    deviation(mv_a[:, :, 0], mv_a[:, :, 1], rn_a[:, :, 0], rn_a[:, :, 1], tmp_a[:, :]).then_inc(a_ln.sem, 2)
                    steps.end()

                def slot_front(self, T, par, n, part):
                    if part != 2:
                        return
                    dve.wait_ge(a_pack.sem, a_pack.ready(2 * T + 1))
                    steps.of(dve.scalar_tensor_tensor(key[:, :], words, 0.0, cst[:, C_BASE:C_BASE + NW], ALU.is_gt, ALU.mult))
                    steps.wait()
                    dve.tensor_tensor(key[:, :], key[:, :], words, ALU.add).then_inc(a_key.sem, 1)
                    dve.wait_ge(a_key.sem, a_key.ready(T))
                    steps.carry()
                    first_bits(key[:, :], 4)
                    steps.of(dve.tensor_copy(topu[:, :], top[:, 0:S]))
                    steps.wait()
                    steps.of(dve.tensor_scalar(hi8[:, :], topu[:, :], 8, 3, ALU.logical_shift_right, ALU.logical_shift_left))
                    steps.of(dve.tensor_tensor(bits[:, :, :], topu[:, :].unsqueeze(2).to_broadcast([P, S, WORD]),
                                               bit_u[:, :].unsqueeze(1).to_broadcast([P, S, WORD]), ALU.bitwise_and))
                    steps.wait()
                    steps.of(dve.tensor_tensor(score[:, :, :], hi8[:, :].unsqueeze(2).to_broadcast([P, S, WORD]),
                                               cst[:, C_R:C_R + WORD].unsqueeze(1).to_broadcast([P, S, WORD]), ALU.subtract))
                    steps.wait()
                    steps.of(dve.scalar_tensor_tensor(score[:, :, :], bits[:, :, :], 0.0, score[:, :, :], ALU.is_gt, ALU.mult))
                    steps.wait()
                    first_bits(key[:, 0:S * WORD], 4)
                    dve.tensor_scalar(idx[:, par, :], top[:, 0:S], -1.0, cst[:, bass.ds(T + C_OFF, 1)], ALU.mult, ALU.add)\
                       .then_inc(idx_ready.sem, 1)
                    dve.wait_ge(idx_ready.sem, idx_ready.ready(T))
                    steps.carry()
                    steps.end()

                def slot_back(self, T, par, n, part, front):
                    if part == 1:
                        dve.wait_ge(gathered[par], 16 * S * n + 16 * S)
                        dve.wait_ge(cat_tr.sem, cat_tr.free(T, 1))
                        dve.tensor_reduce(cat[:, C:2 * C], gath[:, par, :, :].rearrange("p s c -> p c s"), AX, ALU.max)\
                           .then_inc(reduced.sem, 1)
                    if part == 3:
                        dve.wait_ge(o_done.sem, o_done.ready(T))
                        dve.wait_ge(x1_ld, 16 * T + 16)
                        dve.scalar_tensor_tensor(x1[:, :], o_mm, -1.0, x1[:, :], ALU.max, ALU.add).then_inc(x1_done.sem, 1)

                def prep(self, p, b, g):
                    G = NQ * b + g
                    if p == 2:
                        here = bass.ds(BLK * g, BLK)
                        hi, mid, low = split[:, here, 2 * C:3 * C], split[:, here, 0:C], split[:, here, C:2 * C]
                        dve.wait_ge(hi_ok.sem, hi_ok.ready(G))
                        dve.wait_ge(ut_ok.sem, ut_ok.ready(G))
                        steps.of(dve.tensor_tensor(res, acc[:, :, 0:C], hi, ALU.subtract))
                        steps.wait()
                        steps.of(dve.tensor_copy(mid, res))
                        steps.wait()
                        steps.of(dve.tensor_tensor(res, res, mid, ALU.subtract))
                        steps.wait()
                        dve.tensor_copy(low, res).then_inc(ev_ok[2].sem, 1)
                        dve.wait_ge(ev_ok[2].sem, ev_ok[2].ready(G))
                        steps.carry()
                        steps.end()

                def norm(self, p, b):
                    if p == 1:
                        for g in range(NQ):
                            dve.wait_ge(xr_ld, 16 * NQ * b + 16 * g + 16)
                            block_stats(g)
                        steps.wait()
                    if p == 2:
                        steps.of(dve.memset(split[:, :, 3 * C:3 * C + 1], 1.0))
                    for t in range(NT):
                        steps.of(dve.bn_aggr(mv[:, t, :], st[:, t, :]))
                    steps.wait()
                    deviation(mv[:, :, 0], mv[:, :, 1], rs[:, :], nm[:, :], tmp[:, :]).then_inc(ln_ok[p].sem, 1)
                    steps.end()

                def spread(self, p, b):
                    H = heads(p)
                    dve.wait_ge(ev_ok[p].sem, ev_ok[p].ready(NQ * b + NQ - 1))
                    dve.tensor_reduce(dmx[:, 0:H], sd[:, :, H:2 * H].rearrange("p t h -> p h t"), AX, ALU.max).then_inc(gd[p], 1)
                    dve.wait_ge(gp[p], 2 * b + 1)
                    steps.of(dve.tensor_reduce(dtop[0:H, :], psB[0:H, 0:P], AX, ALU.max))
                    steps.wait()
                    dve.tensor_scalar(ddiag[0:H, 0:H], cst[0:H, C_ID:C_ID + H], dtop[0:H, :], None, ALU.mult).then_inc(gd[p], 1)
                    dve.wait_ge(gp[p], 2 * b + 2)
                    D = psB[:, P:P + H].unsqueeze(1).to_broadcast([P, NT, H])
                    steps.of(dve.tensor_tensor(dd[:, :, 0:H], sd[:, :, H:2 * H], D, ALU.subtract))
                    steps.of(dve.tensor_tensor(sp_[:, :, 0:H], sd[:, :, 0:H], D, ALU.add))
                    steps.wait()
                    steps.of(dve.tensor_scalar(sp_[:, :, 0:H], sp_[:, :, 0:H], LIM, None, ALU.min))
                    dve.tensor_scalar(dd[:, :, 0:H], dd[:, :, 0:H], -LIM, None, ALU.max).then_inc(gd[p], 1)
                    dve.wait_ge(ga[p], b + 1)
                    W = C // H + 1
                    vals = V[p].rearrange("p t (h f) -> p t h f", h=H)
                    if H == 1:
                        steps.of(dve.tensor_tensor(vals[:, :, 0, 0:C], vals[:, :, 0, 0:C], vv[:, :, 0:1].to_broadcast([P, NT, C]), ALU.mult))
                    else:
                        flat = region[:, 0:val_cols].rearrange("p (t f) -> p t f", f=W)
                        steps.of(dve.tensor_tensor(flat[:, :, 0:F], flat[:, :, 0:F],
                                                   vv[:, :, :].rearrange("p t h -> p (t h)").unsqueeze(2).to_broadcast([P, NT * H, F]), ALU.mult))
                    steps.of(dve.tensor_copy(vals[:, :, :, W - 1], vv[:, :, 0:H]))
                    steps.end()
                    dve.sem_inc(gd[p], 1)

                def attend_start(self, p, b, q):
                    Q = NQ * b + q
                    dve.tensor_copy(sq[:, :, 0:heads(p)], sp_[:, bass.ds(BLK * q, BLK), 0:heads(p)]).then_inc(sq_ok[p].sem, 1)

                def attend(self, p, b, q, j0, j1):
                    H, Q = heads(p), NQ * b + q
                    for J in range(j0, j1):
                        for h in range(H):
                            n = H * J + h
                            if J == 0:
                                dve.wait_ge(wB_ok[p].sem, wB_ok[p].ready(H * Q + h))
                            dve.wait_ge(mm_ok[p].sem, mm_ok[p].free(NT * H * Q + n, 4))
                            dve.scalar_tensor_tensor(
                                edge[:, n % 4, :], wB[:, h, :], gg[:, J, h:h + 1],
                                adjT[:, J, bass.ds((b % 2) * N + 512 * q, 512)], ALU.max, ALU.mult).then_inc(edge_ok[p].sem, 1)

                def attend_end(self, p, b, q):
                    H, Q = heads(p), NQ * b + q
                    W = C // H + 1
                    dve.wait_ge(mm_ok[p].sem, mm_ok[p].ready(NT * H * Q + NT * H - 1))
                    sums = acc[:, :, 0:H * W].rearrange("p t (h f) -> p t h f", h=H)
                    steps.of(dve.reciprocal(den[:, :, 0:H], sums[:, :, :, W - 1]))
                    steps.wait()
                    here = xr[:, bass.ds(BLK * q, BLK), :]
                    if p == 1:
                        y4 = y_s.rearrange("p t (h f) -> p t h f", h=H)
                        dve.tensor_tensor(y4, sums[:, :, :, 0:F], den[:, :, :].unsqueeze(3).to_broadcast([P, BLK, H, F]), ALU.mult)\
                           .then_inc(y_ok.sem, 1)
                        dve.wait_ge(e_ok.sem, e_ok.ready(Q))
                        steps.of(dve.scalar_tensor_tensor(e_s, e_s, 1.0, here, ALU.min, ALU.add))
                        steps.wait()
                        dve.scalar_tensor_tensor(here, y_s, 0.0, e_s, ALU.max, ALU.add).then_inc(x_ok[p].sem, 1)
                    else:
                        for k in range(BLK):
                            row = xr[:, bass.ds(BLK * q + k, 1), :].rearrange("p t c -> p (t c)")
                            ins = dve.scalar_tensor_tensor(row, acc[:, k, 0:C], den[:, k, 0:1], row, ALU.mult, ALU.add)
                        ins.then_inc(x_ok[p].sem, 1)
                    dve.wait_ge(x_ok[p].sem, x_ok[p].ready(Q))
                    if p == 1:
                        block_stats(q)
                    else:
                        steps.carry()
                    steps.end()

                def mean(self, b, q, k):
                    J = 4 * (NQ * b + q) + k
                    if k == 0:
                        dve.wait_ge(u_ld, 16 * (NQ * b + q) + 16)
                    dve.wait_ge(c_mm.sem, c_mm.ready(4 * J + 3))
                    steps.of(dve.tensor_scalar(den[:, k, 0:1], acc[:, k, C:C + 1], 1.0, None, ALU.max))
                    steps.wait()
                    steps.of(dve.reciprocal(den[:, k, 1:2], den[:, k, 0:1]))
                    steps.wait()
                    steps.of(dve.scalar_tensor_tensor(res[:, k, :], acc[:, k, 0:C], den[:, k, 1:2], u2_s[:, k, :], ALU.mult, ALU.add))
                    steps.wait()
                    row = xr[:, bass.ds(BLK * q + k, 1), :].rearrange("p t c -> p (t c)")
                    dve.scalar_tensor_tensor(row, res[:, k, :], 0.0, row, ALU.max, ALU.add).then_inc(x2_ok.sem, 1)
                    dve.wait_ge(x2_ok.sem, x2_ok.ready(J))
                    if k == BLK - 1:
                        block_stats(q)
                    else:
                        steps.carry()
                    steps.end()

            program(dve, Do())


N_LOADS = 11
_INS = ["x", "adj", "L0_gnn_W", "L0_gnn_b", "L1_gnn_W", "L1_gnn_a_src", "L1_gnn_a_dst", "L2_gnn_W_msg", "L2_gnn_W_upd",
        "L2_gnn_bias", "L3_gnn_W", "L3_gnn_a"]


def kernel(**inputs):
    import numpy as np
    import concourse.bacc as bacc
    from concourse.bass_utils import run_bass_kernel_spmd

    nc = bacc.Bacc("TRN2", target_bir_lowering=False, num_devices=1)
    arrays = {f"in_{n}": np.ascontiguousarray(inputs[n]) for n in _INS}
    arrays["in_const"] = constants()
    args = [nc.dram_tensor(n, a.shape, mybir.dt.from_np(a.dtype), kind="ExternalInput").ap() for n, a in arrays.items()]
    out = nc.dram_tensor("out_0", (B, N, C), F32, kind="ExternalOutput").ap()
    gnn_kernel(nc, *args, out)
    r = run_bass_kernel_spmd(nc, [arrays], core_ids=[0])
    return r.results[0]["out_0"]
```

```python
from contextlib import ExitStack

import concourse.bass as bass
from concourse import mybir

F32 = mybir.dt.float32
BF16 = mybir.dt.bfloat16
I32 = mybir.dt.int32
U32 = mybir.dt.uint32
U8 = mybir.dt.uint8
ALU = mybir.AluOpType
ACT = mybir.ActivationFunctionType
AX = mybir.AxisListType.X

P = 128
B = 8
N = 2048
C = 256
NT = N // P
BLK = 4
NQ = NT // BLK
S = 25
HEADS = 4
F = C // HEADS
WORD = 8
NW = N // WORD
WPT = P // WORD
TAB = N + 1
SLOTS = NT
LAG = 2
EPS = 1e-5
SLOPE = 0.2
LIM = 90.0

C_ID, C_BASE, C_OFF = 0, P, P + NW
C_PACK = C_OFF + B * NT
C_R = C_PACK + WPT
C_BIT = C_R + WORD
C_ONE = C_BIT + WORD
C_END = C_ONE + 1


def constants():
    import numpy as np
    c = np.zeros((P, C_END), np.float32)
    p = np.arange(P)
    c[:, C_ID:C_ID + P] = np.eye(P)
    c[:, C_ONE] = 1.0
    c[:, C_BASE:C_BASE + NW] = (NW - np.arange(NW)) * 256.0
    c[:, C_OFF:C_OFF + B * NT] = N + TAB * (np.arange(B * NT) // NT % 2)
    c[p, C_PACK + p // WORD] = 2.0 ** (WORD - 1 - p % WORD)
    c[:, C_R:C_R + WORD] = np.arange(WORD)
    c[:, C_BIT:C_BIT + WORD] = 2.0 ** (WORD - 1 - np.arange(WORD))
    return c


class Count:

    def __init__(self, sem, credit=0):
        self.sem, self.credit = sem, credit

    def ready(self, n):
        return n + (self.credit + 1)

    def free(self, n, depth):
        assert self.credit >= depth
        return n + (self.credit + 1 - depth)


def gnn_kernel(nc, x, adj, w0, b0, w1, a1s, a1d, w2m, w2u, b2, w3, a3, const, out):
    ctx = ExitStack()
    with ctx:
        def sb(name, shape, dt):
            return ctx.enter_context(nc.sbuf_tensor(name, shape, dt))

        def sem(name):
            return ctx.enter_context(nc.semaphore(name))

        def count(name, credit=0):
            return Count(sem(name), credit)

        htab = nc.dram_tensor("htab", [2 * TAB, C], F32, kind="Internal").ap()
        x1d = nc.dram_tensor("x1d", [B * N, C], F32, kind="Internal").ap()
        u2d = nc.dram_tensor("u2d", [N, C], F32, kind="Internal").ap()
        rows = lambda t: t.rearrange("(t p) c -> p t c", p=P)
        x_r, x1_r, u2_r = rows(x.rearrange("b n c -> (b n) c")), rows(x1d), rows(u2d)
        out_r = rows(out.rearrange("b n c -> (b n) c"))
        adj_r = adj.rearrange("b (i p) j -> p (b i) j", p=P)

        cst = sb("cst", [P, C_END], F32)
        ident, one = cst[:, C_ID:C_ID + P], cst[:, C_ONE:C_ONE + 1]
        ident_bf = sb("ident_bf", [P, P], BF16)
        pack_bf = sb("pack_bf", [P, WPT], BF16)
        bit_u = sb("bit_u", [P, WORD], U32)
        w0_s = sb("w0_s", [P, 4, C], F32)
        w1_s = sb("w1_s", [P, 2, C + 2 * HEADS], F32)
        w2_s = sb("w2_s", [P, 2, 2 * C], F32)
        w3_s = sb("w3_s", [P, 2, C + 2], F32)
        bias = sb("bias", [P // 4 + 1, C], F32)
        adj_i = sb("adj_i", [P, 2, 512], I32)
        adj_b = sb("adj_b", [P, 2, 512], BF16)
        adjT_b = sb("adjT_b", [P, 1024], BF16)
        adjT = sb("adjT", [P, NT, 2 * N], U8)
        key = sb("key", [P, NW], F32)
        top = sb("top", [P, 32], F32)
        topu = sb("topu", [P, S], U32)
        hi8 = sb("hi8", [P, S], U32)
        bits = sb("bits", [P, S, WORD], U32)
        score = key[:, 0:S * WORD].rearrange("p (s r) -> p s r", s=S)
        idx = sb("idx", [P, 2, S], U32)
        gath = sb("gath", [P, 2, S, C], F32)
        cat = sb("cat", [P, 2 * C], F32)
        catT = sb("catT", [P, 4, P], F32)
        x1 = sb("x1", [P, C], F32)
        xa = sb("xa", [P, 2, C], F32)
        st_a = sb("st_a", [P, 2, 6], F32)
        mv_a = sb("mv_a", [P, 2, 2], F32)
        rn_a = sb("rn_a", [P, 2, 2], F32)
        xr = sb("xr", [P, NT, C], F32)
        hb = sb("hb", [P, BLK, C], F32)
        st = sb("st", [P, NT, 6], F32)
        mv = sb("mv", [P, NT, 2], F32)
        rs = sb("rs", [P, NT], F32)
        nm = sb("nm", [P, NT], F32)
        tmp = sb("tmp", [P, NT], F32)
        tmp_a = sb("tmp_a", [P, 2], F32)
        sd = sb("sd", [P, NT, 2 * HEADS], F32)
        dmx = sb("dmx", [P, HEADS], F32)
        dtop = sb("dtop", [HEADS, 1], F32)
        ddiag = sb("ddiag", [HEADS, HEADS], F32)
        dd = sb("dd", [P, NT, HEADS], F32)
        sp_ = sb("sp_", [P, NT, HEADS], F32)
        vv = sb("vv", [P, NT, HEADS], F32)
        gg = sb("gg", [P, NT, HEADS], F32)
        sq = sb("sq", [P, BLK], F32)
        den = sb("den", [P, BLK, HEADS], F32)
        col_i = sb("col_i", [P, 2, 4, P], I32)
        hb_f = hb[:, :, :].rearrange("p a c -> p (a c)")
        col_f = col_i[:, :, :, :].rearrange("p m i j -> p (m i j)").bitcast(F32)
        hb_i = hb_f.bitcast(I32).rearrange("p (m i j) -> p m i j", m=2, i=4)
        cols = [col_i[:, 0, :, :], col_i[:, 1, :, :], hb_i[:, 0, :, :], hb_i[:, 1, :, :]]
        col_b = sb("col_b", [P, 2, 4, P], BF16)
        ye = col_b[:, :, :, :].rearrange("p m i j -> p (m i j)").bitcast(F32)
        val_cols = NT * HEADS * (F + 1)
        region = sb("region", [P, val_cols + HEADS * 512], F32)
        V = {1: region[:, 0:val_cols].rearrange("p (t c) -> p t c", t=NT),
             3: region[:, 0:NT * (C + 1)].rearrange("p (t c) -> p t c", t=NT)}
        wB = region[:, val_cols:val_cols + HEADS * 512].rearrange("p (h i) -> p h i", h=HEADS)
        SPL = 3 * C + 2
        split = region[:, 0:NT * SPL // 2].bitcast(BF16).rearrange("p (t c) -> p t c", t=NT)
        edge = sb("edge", [P, 4, 512], F32)
        edge_f = edge[:, :, :].rearrange("p a c -> p (a c)")
        hT = edge_f[:, 0:1024].rearrange("p (t k r) -> p t k r", t=BLK, k=2)
        res = edge_f[:, 1024:2048].rearrange("p (t c) -> p t c", t=BLK)
        u2_s = edge_f[:, 0:1024].rearrange("p (t c) -> p t c", t=BLK)

        yT = [hb_f[0:F + 1, 0:512], hb_f[0:F + 1, 512:1024], col_f[0:F + 1, 0:512], col_f[0:F + 1, 512:1024]]

        def result_of(q, k):
            if q == NQ - 1:
                return edge_f[:, C * k:C * k + C], edge_f[:, C * (BLK + k):C * (BLK + k) + C]
            return ye[:, 0:C], ye[:, C:2 * C]

        def pb(name, shape, dt):
            return ctx.enter_context(nc.psum_tensor(name, shape, dt))

        acc = pb("acc", [P, BLK, 512], F32)
        psT = pb("psT", [P, 1024], BF16)
        psH = pb("psH", [P, 512], F32)
        psO = pb("psO", [P, 512], F32)
        psB = pb("psB", [P, 512], F32)
        o_mm, words = psO[:, 0:C], psO[:, C:2 * C]

        w_ld, w_cast, w_red, w_tr, w_ev, w_done = (sem(n) for n in ("w_ld", "w_cast", "w_red", "w_tr", "w_ev", "w_done"))
        tiles_begun, loads_begun = sem("tiles_begun"), sem("loads_begun")
        zero_st, zero_set = sem("zero_st"), sem("zero_set")
        chain = sem("chain")
        a_ld = [sem("a_ld0"), sem("a_ld1")]
        a_cast, a_used = count("a_cast", 2), count("a_used", 2)
        a_evac, a_pack = count("a_evac", 1), count("a_pack", 1)
        a_key, idx_ready, reduced = count("a_key", 1), count("idx_ready"), count("reduced", 2)
        gathered = [sem("gathered0"), sem("gathered1")]
        xa_ld = [sem("xa_ld0"), sem("xa_ld1")]
        a_ln, a_relu = count("a_ln"), count("a_relu", 2)
        h_dma, h_stored = sem("h_dma"), count("h_stored")
        cat_ld, x1_ld = sem("cat_ld"), sem("x1_ld")
        cat_tr, cat_ev, o_done, x1_done = (count(n, m) for n, m in (("cat_tr", 1), ("cat_ev", 1), ("o_done", 1), ("x1_done", 3)))
        x1_dma, x1_stored = sem("x1_dma"), count("x1_stored")
        xr_ld = sem("xr_ld")
        ln_ok = {p: count(f"ln{p}") for p in (1, 2, 3)}
        h_ok = {p: count(f"h{p}", 1) for p in (1, 2, 3)}
        tp_ok = {p: count(f"tp{p}", 1) for p in (1, 2, 3)}
        hT_ok = {p: count(f"hT{p}") for p in (1, 2, 3)}
        dn_ok = {p: count(f"dn{p}", 1) for p in (1, 2, 3)}
        ev_ok = {p: count(f"ev{p}", 1) for p in (1, 2, 3)}
        hi_ok, ut_ok, u_dma, u_stored = count("hi_ok"), count("ut_ok", 1), sem("u_dma"), count("u_stored", 1)
        gd = {p: sem(f"gd{p}") for p in (1, 3)}
        gp = {p: sem(f"gp{p}") for p in (1, 3)}
        ga = {p: sem(f"ga{p}") for p in (1, 3)}
        sq_ok = count("sq_ok")
        sB_ok = {p: count(f"sB{p}") for p in (1, 3)}
        wB_ok = {p: count(f"wB{p}", 1) for p in (1, 3)}
        edge_ok = {p: count(f"edge{p}", 4) for p in (1, 3)}
        mm_ok = {p: count(f"mm{p}", 4) for p in (1, 3)}
        x3_ok = count("x3_ok", 1)
        yT_ok, back_ok, y_ok, e_ok = count("yT_ok", 4), count("back_ok"), count("y_ok", 1), count("e_ok")
        out_st = sem("out_st")
        c_ld = [sem(f"c_ld{m}") for m in range(4)]
        c_cast, c_mm, x2_ok, u_ld = count("c_cast", 4), count("c_mm", 2), count("x2_ok", 4), sem("u_ld")

        def front_tile(b, sh, par):
            return 16 * (b + 1) + LAG + 2 * sh + par

        def back_tile(b, sh, par):
            return 16 * (b + 1) + 2 * sh + par

        def half(b, sh):
            return 8 * (b + 1) + sh

        PARTS = 8
        PLAN = [("prep1", 1), ("attend1", 1), ("prep2", 1), ("mean", 2), ("prep3", 1), ("attend3", 2)]
        LOOPED = ("mean", "attend3")
        assert 2 * sum(n for _, n in PLAN) == SLOTS

        def body(eng, b, do, front=lambda s: True, pre=True, slots=True, unroll_last=False):
            def steps_of(phase, q):
                if phase.startswith("prep"):
                    return [lambda part=part: do.prep(int(phase[-1]), b, q, part) for part in range(3)]
                if phase == "mean":
                    return [lambda k=k, m=m: do.mean(b, q, k, m) for k in range(BLK) for m in range(4)]
                p = int(phase[-1])
                steps = [lambda J=J: do.attend(p, b, q, J) for J in range(NT)]
                if p == 3:
                    return [lambda: do.attend_start(3, b, q)] + steps + [lambda: do.attend_end(3, b, q)]
                if q == 0:
                    return [lambda: do.attend_start(1, b, 0)] + steps + [lambda: do.attend_end(1, b, 0)]
                for k in range(BLK):
                    steps.insert(5 * k + 2, lambda k=k: do.result(b, q - 1, k))
                    steps.insert(5 * k + 4, lambda k=k: do.add(b, q - 1, k))
                steps.append(lambda: do.attend_end(1, b, q))
                if q == NQ - 1:
                    tail = [(do.result, 0)] + [(f, k) for k in range(1, BLK) for f, k in ((do.result, k), (do.add, k - 1))] + [(do.add, BLK - 1)]
                    steps += [lambda f=f, k=k: f(b, q, k) for f, k in tail]
                return steps

            def pair(phase, r, n, s0, pre_0):
                main, then = steps_of(phase, 2 * r), steps_of(phase, 2 * r + 1)
                if phase == "attend3":
                    main.insert(len(main) - 1, then.pop(0))
                main += then
                side = []
                for i in range(n if slots else 0):
                    sh, par = s0(i)
                    k = None if pre_0 is None or not pre else pre_0 + i
                    side += [lambda part=part, sh=sh, par=par, k=k: do.slot(b, sh, par, part, front, k) for part in range(PARTS)]
                done = 0
                for i, step in enumerate(main):
                    while done * len(main) < (i + 1) * len(side) and done < len(side):
                        side[done]()
                        done += 1
                    step()

            s = pre_done = 0
            for phase, n in PLAN:
                if phase.startswith("prep"):
                    p = int(phase[-1])
                    if p == 1:
                        do.fetch(b)
                    do.norm(p, b)
                if phase == "mean":
                    do.mean_start(b)
                if phase not in LOOPED:
                    for r in range(NQ // 2):
                        pair(phase, r, n, lambda i: ((s + n * r + i) // 2, (s + n * r + i) % 2), pre_done + n * r)
                    pre_done += 2 * n
                elif unroll_last and s + 2 * n == SLOTS:
                    for r in range(NQ // 2):
                        pair(phase, r, n, lambda i: ((s + n * r + i) // 2, (s + n * r + i) % 2), None)
                else:
                    with eng.Fori(0, NQ // 2) as r:
                        pair(phase, r, n, lambda i: (r * (n // 2) + (s + i) // 2, i % 2), None)
                s += 2 * n
                if phase in ("prep1", "prep3"):
                    do.spread(int(phase[-1]), b)
            assert pre_done == NT // 2
            do.end(b)

        def program(eng, do):
            do.setup()
            with eng.Fori(0, NT // 2) as i:
                for part in range(PARTS):
                    do.pre(2 * i, i, part)
            do.ahead(0, PARTS - 2)
            for T in range(LAG):
                for part in range(PARTS):
                    do.slot_front(T, T, 0, part)
                    do.ahead(T + 1, part)
            for first in (0, 4):
                with eng.Fori(first, first + 4) as sh:
                    for par in range(2):
                        for part in range(PARTS):
                            do.slot(-1, sh, par, part, lambda s: True, 2 * sh + par if first == 0 else None)
            with eng.Fori(0, B - 2) as b:
                body(eng, b, do)
            body(eng, B - 2, do, front=lambda s: s < SLOTS - LAG, pre=False, unroll_last=True)
            body(eng, B - 1, do, slots=False)

        class Part:
            def setup(self): pass
            def pre(self, u, n, part): pass
            def slot_front(self, T, par, n, part): pass
            def slot_back(self, T, par, n, part, front): pass
            def prep(self, p, b, g, part): pass
            def spread(self, p, b): pass
            def attend_start(self, p, b, q): pass
            def attend(self, p, b, q, J): pass
            def attend_end(self, p, b, q): pass
            def result(self, b, q, k): pass
            def add(self, b, q, k): pass
            def fetch(self, b): pass
            def norm(self, p, b): pass
            def ahead(self, T, part): pass
            def mean_start(self, b): pass
            def mean(self, b, q, k, m): pass
            def end(self, b): pass

            def slot(self, b, sh, par, part, front, k):
                known = isinstance(sh, int)
                enters = not known or front(2 * sh + par)
                next_enters = not known or front(2 * sh + par + 1)
                Tf, Tb, n = front_tile(b, sh, par), back_tile(b, sh, par), half(b, sh)
                if part == 0:
                    self.slot_back(Tb, par, n, part, enters)
                if enters:
                    self.slot_front(Tf, par, n + LAG // 2, part)
                if k is not None:
                    self.pre(16 * (b + 2) + 2 * k, 8 * (b + 2) + k, part)
                if part != 0:
                    self.slot_back(Tb, par, n, part, enters)
                if next_enters:
                    self.ahead(Tf + 1, part)

        def table_row(T):
            return (T % (2 * NT)) * P + (T % (2 * NT)) // NT

        def heads(p):
            return HEADS if p == 1 else 1

        block = ctx.enter_context(nc.Block())

        @block.sync
        def _(sp):
            class Do(Part):
                def setup(self):
                    sp.sem_inc(u_stored.sem, u_stored.credit)
                    kp = "(k p) n -> p k n"
                    tmp = gath[:, 0, :, :]
                    loads = [
                        (cst[:, :], const), (w0_s[:, :, :], w0.rearrange(kp, p=P)),
                        (w1_s[:, :, 0:C], w1.rearrange(kp, p=P)),
                        (w2_s[:, :, 0:C], w2m.rearrange(kp, p=P)), (w2_s[:, :, C:2 * C], w2u.rearrange(kp, p=P)),
                        (tmp[:, 0:2, :], w3.rearrange(kp, p=P)),
                        (tmp[:, 2, :], a1s.rearrange("h f -> (h f)").partition_broadcast(P)),
                        (tmp[:, 3, :], a1d.rearrange("h f -> (h f)").partition_broadcast(P)),
                        (tmp[:, 4:6, :], a3.rearrange("a (k c) -> (a k) c", k=2).partition_broadcast(P)),
                        (bias[0:1, :], b0.rearrange("(a c) -> a c", a=1)),
                        (bias[32:33, :], b2.rearrange("(a c) -> a c", a=1)),
                    ]
                    assert len(loads) == N_LOADS
                    for to, fr in loads:
                        sp.dma_start(to, fr).then_inc(w_ld, 16)
                    sp.wait_ge(zero_set, 1)
                    for i in range(2):
                        sp.dma_start(htab[i * N:i * N + N, :].rearrange("(p t) c -> p (t c)", p=P), xr[:, :, :].rearrange("p t c -> p (t c)")).then_inc(zero_st, 16)
                    sp.dma_start(htab[2 * N:2 * TAB, :], xr[0:2, 0, :]).then_inc(zero_st, 16)
                    sp.wait_ge(zero_st, 48)

                def pre(self, u, n, part):
                    if part == 0:
                        for i in range(2):
                            sp.dma_start(xa[:, i, :], x_r[:, bass.ds(u + i, 1), :].rearrange("p t c -> p (t c)")).then_inc(xa_ld[i], 16)
                    if part == 7:
                        for i in range(2):
                            sp.wait_ge(a_relu.sem, a_relu.ready(u + i))
                            sp.dma_start(htab[bass.ds(table_row(u + i), P), :], xa[:, i, :]).then_inc(h_dma, 16)
                        sp.wait_ge(h_dma, 16 * (u + 1) + 16)
                        sp.sem_inc(h_stored.sem, 2)

                def quarters(self, T, first):
                    for k in range(first, first + 2):
                        sp.wait_ge(a_cast.sem, a_cast.free(4 * T + k, 2))
                        sp.dma_start(adj_i[:, k % 2, :], adj_r[:, bass.ds(T, 1), 512 * k:512 * k + 512].rearrange("p t c -> p (t c)")).then_inc(a_ld[k % 2], 16)

                def ahead(self, T, part):
                    if part == 6:
                        self.quarters(T, 0)

                def slot_front(self, T, par, n, part):
                    if part == 1:
                        self.quarters(T, 2)

                def slot_back(self, T, par, n, part, front):
                    if part == 0:
                        sp.wait_ge(cat_tr.sem, cat_tr.free(T, 1))
                        sp.dma_start(cat[:, 0:C], htab[bass.ds(table_row(T), P), :]).then_inc(cat_ld, 16)
                        sp.dma_start(x1[:, :], x_r[:, bass.ds(T, 1), :].rearrange("p t c -> p (t c)")).then_inc(x1_ld, 16)
                    if part == 7:
                        sp.wait_ge(x1_done.sem, x1_done.ready(T))
                        sp.dma_start(x1_r[:, bass.ds(T, 1), :].rearrange("p t c -> p (t c)"), x1[:, :]).then_inc(x1_dma, 16)
                        sp.wait_ge(x1_dma, 16 * T + 16)
                        sp.sem_inc(x1_stored.sem, 1)

                def fetch(self, b):
                    for g in range(NQ):
                        sp.dma_start(xr[:, BLK * g:BLK * g + BLK, :], x1_r[:, bass.ds(NT * b + BLK * g, BLK), :]).then_inc(xr_ld, 16)
                        sp.wait_ge(xr_ld, 16 * (NQ * b + g) + 16)
                        sp.sem_inc(loads_begun, 1)

                def prep(self, p, b, g, part):
                    G = NQ * b + g
                    if p == 2 and part == 2:
                        sp.wait_ge(ut_ok.sem, ut_ok.ready(G))
                        sp.dma_start(u2_r[:, bass.ds(BLK * g, BLK), :], hb[:, :, :]).then_inc(u_dma, 16)
                        sp.wait_ge(u_dma, 16 * G + 16)
                        sp.sem_inc(u_stored.sem, 1)

                def mean_start(self, b):
                    sp.wait_ge(ev_ok[2].sem, ev_ok[2].ready(NQ * b + NQ - 1))
                    sp.sem_inc(loads_begun, 1)

                def mean(self, b, q, k, m):
                    J = 4 * (NQ * b + q) + k
                    sp.wait_ge(c_cast.sem, c_cast.free(4 * J + m, 4))
                    sp.dma_start(cols[m], adj_r[:, bass.ds(NT * b + 4 * m, 4), bass.ds((4 * q + k) * P, P)]).then_inc(c_ld[m], 16)
                    if k == 0 and m == 2:
                        sp.wait_ge(x2_ok.sem, x2_ok.free(J + 3, 4))
                        sp.dma_start(u2_s, u2_r[:, bass.ds(BLK * q, BLK), :]).then_inc(u_ld, 16)

                def attend_end(self, p, b, q):
                    if p == 3:
                        Q = NQ * b + q
                        sp.wait_ge(x3_ok.sem, x3_ok.ready(Q))
                        sp.dma_start(out_r[:, bass.ds(BLK * Q, BLK), :], xr[:, bass.ds(BLK * q, BLK), :]).then_inc(out_st, 16)

                def end(self, b):
                    sp.wait_ge(out_st, 16 * NQ * (b + 1))
                    sp.sem_inc(loads_begun, 1)

            program(sp, Do())

        @block.gpsimd
        def _(pool):
            class Do(Part):
                def slot_front(self, T, par, n, part):
                    if part != 5:
                        return
                    pool.wait_ge(h_stored.sem, (T // NT) * NT + NT)
                    pool.wait_ge(reduced.sem, reduced.free(T, 2))
                    pool.wait_ge(idx_ready.sem, idx_ready.ready(T))
                    pool.sem_inc(tiles_begun, 1)
                    for s in range(S):
                        pool.indirect_dma_start(
                            out=gath[:, par, s, :], out_offset=None, in_=htab,
                            in_offset=bass.IndirectOffsetOnAxis(ap=idx[:, par, s:s + 1], axis=0),
                        ).then_inc(gathered[par], 16)

            program(pool, Do())

        @block.scalar
        def _(act):
            class Do(Part):
                def setup(self):
                    for c in (a_cast, a_evac, a_relu, cat_ev, h_ok[1], h_ok[2], h_ok[3], ev_ok[1], ev_ok[3], ut_ok, wB_ok[1], wB_ok[3], yT_ok, c_cast):
                        act.sem_inc(c.sem, c.credit)
                    act.wait_ge(w_ld, 16 * N_LOADS)
                    act.activation(ident_bf[:, :], ident, ACT.Copy).then_inc(w_cast, 1)
                    act.activation(pack_bf[:, :], cst[:, C_PACK:C_PACK + WPT], ACT.Copy).then_inc(w_cast, 1)
                    act.wait_ge(w_tr, 1)
                    act.activation(w3_s[:, :, 0:C], psH[:, :].rearrange("p (k o) -> p k o", k=2), ACT.Copy).then_inc(w_ev, 1)

                def pre(self, u, n, part):
                    if part == 6:
                        for i in range(2):
                            act.wait_ge(a_ln.sem, a_ln.ready(u + i))
                            act.activation(xa[:, i, :], xa[:, i, :], ACT.Relu, bias=rn_a[:, i, 1:2], scale=rn_a[:, i, 0:1]).then_inc(a_relu.sem, 1)

                def slot_front(self, T, par, n, part):
                    def cast(k):
                        act.wait_ge(a_ld[k % 2], 32 * T + 16 * (k // 2) + 16)
                        act.wait_ge(a_used.sem, a_used.free(4 * T + k, 2))
                        act.activation(adj_b[:, k % 2, :], adj_i[:, k % 2, :], ACT.Copy).then_inc(a_cast.sem, 1)

                    def evacuate(half):
                        act.wait_ge(a_used.sem, a_used.ready(4 * T + 2 * half + 1))
                        act.wait_ge(a_pack.sem, a_pack.free(2 * T + half, 1))
                        act.activation(adjT_b[:, :], psT[:, :], ACT.Copy)
                        act.activation(adjT[:, 8 * half:8 * half + 8, bass.ds((T % (2 * NT)) * P, P)],
                                       psT[:, :].rearrange("p (j i) -> p j i", j=8), ACT.Copy).then_inc(a_evac.sem, 1)

                    if part == 0:
                        cast(0)
                        cast(1)
                    if part == 1:
                        evacuate(0)
                        cast(2)
                        cast(3)
                    if part == 2:
                        evacuate(1)

                def slot_back(self, T, par, n, part, front):
                    if part == 5:
                        act.wait_ge(cat_tr.sem, cat_tr.ready(T))
                        act.wait_ge(o_done.sem, o_done.free(T, 1))
                        act.activation(catT[:, :, :].rearrange("p k r -> p (k r)"), psH[:, :], ACT.Copy).then_inc(cat_ev.sem, 1)

                def relu(self, p, b, g):
                    G = NQ * b + g
                    act.wait_ge(ln_ok[p].sem, ln_ok[p].ready(b))
                    act.wait_ge(tp_ok[p].sem, tp_ok[p].free(G, 1))
                    if p == 2:
                        act.wait_ge(u_stored.sem, u_stored.free(G, 1))
                    for k in range(BLK):
                        ins = act.activation(hb[:, k, :], xr[:, BLK * g + k, :], ACT.Relu,
                                             bias=nm[:, BLK * g + k:BLK * g + k + 1], scale=rs[:, BLK * g + k:BLK * g + k + 1])
                    ins.then_inc(h_ok[p].sem, 1)

                def prep(self, p, b, g, part):
                    G = NQ * b + g
                    ahead = p != 2
                    if part == 0 and (g == 0 or not ahead):
                        self.relu(p, b, g)
                    if part == 1:
                        act.wait_ge(tp_ok[p].sem, tp_ok[p].ready(G))
                        act.wait_ge(dn_ok[p].sem, dn_ok[p].free(G, 1))
                        for k in range(2):
                            ins = act.activation(edge_f[:, 512 * k:512 * k + 512], acc[:, k, :], ACT.Copy)
                        ins.then_inc(hT_ok[p].sem, 1)
                        if ahead and g < NQ - 1:
                            self.relu(p, b, g + 1)
                    if part != 2:
                        return
                    act.wait_ge(dn_ok[p].sem, dn_ok[p].ready(G))
                    if p == 2:
                        act.activation(split[:, BLK * g:BLK * g + BLK, 2 * C:3 * C], acc[:, :, 0:C], ACT.Copy).then_inc(hi_ok.sem, 1)
                        act.activation(hb[:, :, :], acc[:, :, C:2 * C], ACT.Copy).then_inc(ut_ok.sem, 1)
                        return
                    H = heads(p)
                    D = C // H
                    for k in range(BLK):
                        to = V[p][:, BLK * g + k, :].rearrange("p (h f) -> p h f", h=H)[:, :, 0:D]
                        act.activation(to, acc[:, k, 0:C].rearrange("p (h f) -> p h f", h=H), ACT.Copy)
                    act.activation(sd[:, BLK * g:BLK * g + BLK, 0:2 * H], acc[:, :, C:C + 2 * H], ACT.Copy).then_inc(ev_ok[p].sem, 1)

                def spread(self, p, b):
                    H = heads(p)
                    act.wait_ge(gd[p], 4 * b + 3)
                    act.activation(vv[:, :, 0:H], dd[:, :, 0:H], ACT.Exp)
                    act.activation(gg[:, :, 0:H], dd[:, :, 0:H], ACT.Exp, scale=-(1 - SLOPE)).then_inc(ga[p], 1)

                def row_weights(self, p, b, q, h):
                    H, Q = heads(p), NQ * b + q
                    act.wait_ge(edge_ok[p].sem, edge_ok[p].ready(NT * H * Q - H + h))
                    act.wait_ge(sB_ok[p].sem, sB_ok[p].ready(H * Q + h))
                    act.activation(wB[:, h, :], psB[:, :], ACT.Exp, scale=1 - SLOPE).then_inc(wB_ok[p].sem, 1)

                def attend_start(self, p, b, q):
                    for h in range(heads(p)):
                        self.row_weights(p, b, q, h)

                def attend(self, p, b, q, J):
                    if p == 1 and J == NT - 1 and q < NQ - 1:
                        self.attend_start(1, b, q + 1)

                def attend_end(self, p, b, q):
                    if p == 1:
                        Q = NQ * b + q
                        for h in range(HEADS):
                            act.wait_ge(mm_ok[1].sem, mm_ok[1].ready(NT * HEADS * Q + NT * HEADS - HEADS + h))
                            act.wait_ge(y_ok.sem, y_ok.free(BLK * Q, 1))
                            act.activation(yT[h], acc[0:F + 1, h, :], ACT.Copy).then_inc(yT_ok.sem, 1)

                def result(self, b, q, k):
                    y, e = result_of(q, k)
                    n = BLK * (NQ * b + q) + k
                    act.wait_ge(y_ok.sem, y_ok.ready(n))
                    act.activation(e, y, ACT.Exp).then_inc(e_ok.sem, 1)

                def mean(self, b, q, k, m):
                    J = 4 * (NQ * b + q) + k
                    act.wait_ge(c_ld[m], 16 * J + 16)
                    act.wait_ge(c_mm.sem, c_mm.free(4 * J + m, 2))
                    act.activation(col_b[:, m % 2, :, :], cols[m], ACT.Copy).then_inc(c_cast.sem, 1)

            program(act, Do())

        @block.tensor
        def _(pe):
            class Do(Part):
                def setup(self):
                    for c in (a_used, a_pack, cat_tr, o_done, tp_ok[1], tp_ok[2], tp_ok[3], dn_ok[1], dn_ok[2], dn_ok[3], mm_ok[1], mm_ok[3], c_mm):
                        pe.sem_inc(c.sem, c.credit)
                    pe.wait_ge(w_ld, 16 * N_LOADS)
                    for dk in range(2):
                        for ok in range(2):
                            ins = pe.transpose(psH[:, dk * C + ok * P:dk * C + ok * P + P], gath[:, 0, ok, dk * P:dk * P + P], ident)
                    ins.then_inc(w_tr, 1)
                    pe.wait_ge(w_cast, 2)
                    pe.wait_ge(w_done, 1)

                def slot_front(self, T, par, n, part):
                    def turn(half):
                        pe.wait_ge(a_evac.sem, a_evac.free(2 * T + half, 1))
                        for k in range(2):
                            pe.wait_ge(a_cast.sem, a_cast.ready(4 * T + 2 * half + k))
                            for j in range(4):
                                ins = pe.transpose(psT[:, 512 * k + P * j:512 * k + P * j + P], adj_b[:, k, P * j:P * j + P], ident_bf[:, :])
                            ins.then_inc(a_used.sem, 1)

                    def pack(half):
                        pe.wait_ge(a_evac.sem, a_evac.ready(2 * T + half))
                        if half == 0:
                            pe.wait_ge(a_key.sem, a_key.free(T, 1))
                            pe.wait_ge(x1_done.sem, x1_done.ready(T - LAG - 1))
                        for j in range(8):
                            w = WPT * (8 * half + j)
                            ins = pe.matmul(words[:, w:w + WPT], adjT_b[:, P * j:P * j + P], pack_bf[:, :], start=True, stop=True)
                        ins.then_inc(a_pack.sem, 1)

                    if part == 1:
                        turn(0)
                    if part == 2:
                        pack(0)
                        turn(1)
                    if part == 3:
                        pack(1)

                def slot_back(self, T, par, n, part, front):
                    if part == 5:
                        pe.wait_ge(cat_ld, 16 * T + 16)
                        pe.wait_ge(reduced.sem, reduced.ready(T))
                        pe.wait_ge(cat_ev.sem, cat_ev.free(T, 1))
                        for k in range(4):
                            ins = pe.transpose(psH[:, P * k:P * k + P], cat[:, P * k:P * k + P], ident)
                        ins.then_inc(cat_tr.sem, 1)
                    if part == 6:
                        pe.wait_ge(x1_done.sem, x1_done.free(T, 1))
                        if front:
                            pe.wait_ge(a_key.sem, a_key.ready(T + LAG))
                        pe.matmul(o_mm, one[0:1, :].to_broadcast([1, P]), bias[0:1, :], start=True, stop=False)
                        pe.wait_ge(cat_ev.sem, cat_ev.ready(T))
                        for k in range(4):
                            ins = pe.matmul(o_mm, catT[:, k, :], w0_s[:, k, :], start=False, stop=(k == 3))
                        ins.then_inc(o_done.sem, 1)

                def prep(self, p, b, g, part):
                    G = NQ * b + g
                    if part == 0:
                        self.turn_h(p, b, g)
                    if part == 1:
                        self.products(p, b, g)

                def turn_h(self, p, b, g):
                    G = NQ * b + g
                    pe.wait_ge(h_ok[p].sem, h_ok[p].ready(G))
                    pe.wait_ge(ev_ok[p].sem, ev_ok[p].free(G, 1))
                    if p == 2:
                        pe.wait_ge(ut_ok.sem, ut_ok.free(G, 1))
                    for k in range(BLK):
                        for c in range(2):
                            at = (k % 2) * C + c * P
                            ins = pe.transpose(acc[:, k // 2, at:at + P], hb[:, k, c * P:c * P + P], ident)
                    ins.then_inc(tp_ok[p].sem, 1)

                def products(self, p, b, g):
                    G = NQ * b + g
                    pe.wait_ge(hT_ok[p].sem, hT_ok[p].ready(G))
                    w = {1: w1_s, 2: w2_s, 3: w3_s}[p]
                    n = w.shape[2]
                    for k in range(BLK):
                        for c in range(2):
                            ins = pe.matmul(acc[:, k, 0:n], hT[:, k, c, :], w[:, c, :], start=(c == 0), stop=(c == 1 and p != 2),
                                            skip_group_check=True)
                        if p == 2:
                            ins = pe.matmul(acc[:, k, C:2 * C], one[32:33, :].to_broadcast([1, P]), bias[32:33, :], start=False, stop=True,
                                            skip_group_check=True)
                    ins.then_inc(dn_ok[p].sem, 1)

                def spread(self, p, b):
                    H = heads(p)
                    pe.wait_ge(gd[p], 4 * b + 1)
                    pe.transpose(psB[0:H, 0:P], dmx[:, 0:H], ident).then_inc(gp[p], 1)
                    pe.wait_ge(gd[p], 4 * b + 2)
                    pe.matmul(psB[:, P:P + H], one[0:H, :].to_broadcast([H, P]), ddiag[0:H, 0:H], start=True, stop=True).then_inc(gp[p], 1)

                def spread_row(self, p, b, q, h):
                    n = heads(p) * (NQ * b + q) + h
                    pe.wait_ge(wB_ok[p].sem, wB_ok[p].free(n, 1))
                    for k in range(BLK):
                        col = sp_[:, BLK * q + k, h:h + 1] if p == 1 else sq[:, k:k + 1]
                        ins = pe.matmul(psB[:, P * k:P * k + P], col.to_broadcast([P, P]), ident, start=True, stop=True)
                    ins.then_inc(sB_ok[p].sem, 1)

                def attend_start(self, p, b, q):
                    if p == 1:
                        pe.wait_ge(gd[1], 4 * b + 3)
                        pe.wait_ge(y_ok.sem, y_ok.free(BLK * (NQ * b + q), 1))
                    else:
                        pe.wait_ge(sq_ok.sem, sq_ok.ready(NQ * b + q))
                    for h in range(heads(p)):
                        self.spread_row(p, b, q, h)

                def attend(self, p, b, q, J):
                    H, Q = heads(p), NQ * b + q
                    if J == 0:
                        pe.wait_ge(gd[p], 4 * b + 4)
                    if p == 3 and J == 0:
                        pe.wait_ge(x3_ok.sem, x3_ok.free(Q, 1))
                    ahead = p == 1 and J == NT - 1 and q < NQ - 1
                    if ahead:
                        pe.wait_ge(y_ok.sem, y_ok.free(BLK * Q, 1))
                    for h in range(H):
                        n = H * J + h
                        if ahead:
                            self.spread_row(1, b, q + 1, h)
                        if p == 1 and J == 0:
                            pe.wait_ge(yT_ok.sem, yT_ok.free(H * Q + h, H))
                        pe.wait_ge(edge_ok[p].sem, edge_ok[p].ready(NT * H * Q + n))
                        if p == 1:
                            ins = pe.matmul(acc[0:F + 1, h, :], V[1][:, J, (F + 1) * h:(F + 1) * (h + 1)], edge[:, n % 4, :],
                                            start=(J == 0), stop=(J == NT - 1), skip_group_check=True)
                        else:
                            for k in range(BLK):
                                ins = pe.matmul(acc[:, k, 0:C + 1], edge[:, n % 4, P * k:P * k + P], V[3][:, J, :],
                                                start=(J == 0), stop=(J == NT - 1), skip_group_check=True)
                        ins.then_inc(mm_ok[p].sem, 1)

                def result(self, b, q, k):
                    Q = NQ * b + q
                    if k == 0:
                        pe.wait_ge(yT_ok.sem, yT_ok.ready(HEADS * Q + HEADS - 1))
                        if q < NQ - 1:
                            pe.wait_ge(wB_ok[1].sem, wB_ok[1].ready(HEADS * Q + 2 * HEADS - 1))
                    pe.wait_ge(y_ok.sem, y_ok.free(BLK * Q + k, 1))
                    for h in range(HEADS):
                        ins = pe.transpose(psB[:, (F + 1) * h:(F + 1) * (h + 1)], yT[h][:, P * k:P * k + P], ident[0:F + 1, 0:F + 1])
                    ins.then_inc(back_ok.sem, 1)

                def mean(self, b, q, k, m):
                    J = 4 * (NQ * b + q) + k
                    if m == 0:
                        if k == 0:
                            pe.wait_ge(ev_ok[2].sem, ev_ok[2].ready(NQ * b + NQ - 1))
                        pe.wait_ge(x2_ok.sem, x2_ok.free(J, 4))
                    pe.wait_ge(c_cast.sem, c_cast.ready(4 * J + m))
                    for i in range(4):
                        t = 4 * m + i
                        w = col_b[:, m % 2, i, :]
                        pe.matmul(acc[:, k, 0:C + 1], w, split[:, t, 2 * C:3 * C + 1], start=(t == 0), stop=False, skip_group_check=True)
                        pe.matmul(acc[:, k, 0:C], w, split[:, t, 0:C], start=False, stop=False, skip_group_check=True)
                        ins = pe.matmul(acc[:, k, 0:C], w, split[:, t, C:2 * C], start=False, stop=(t == NT - 1), skip_group_check=True)
                    ins.then_inc(c_mm.sem, 1)

            program(pe, Do())

        @block.vector
        def _(dve):
            class Steps:
                n = 0

                def of(self, ins):
                    ins.then_inc(chain, 1)
                    self.n += 1

                def wait(self):
                    dve.wait_ge(chain, self.n)

                def carry(self):
                    dve.sem_inc(chain, 1)
                    self.n += 1

                def end(self):
                    self.wait()
                    dve.sem_clear(chain)
                    self.n = 0

            steps = Steps()

            def deviation(mean, var, rstd, shift, tmp):
                steps.of(dve.tensor_scalar(var, var, EPS, None, ALU.add))
                steps.wait()
                steps.of(dve.tensor_scalar(tmp.bitcast(U32), var.bitcast(U32), 1, None, ALU.logical_shift_right))
                steps.wait()
                steps.of(dve.tensor_scalar(rstd.bitcast(U32), tmp.bitcast(U32), -1.0, float(0x5F3759DF), ALU.mult, ALU.add))
                for _ in range(3):
                    steps.wait()
                    steps.of(dve.scalar_tensor_tensor(tmp, rstd, -0.5, rstd, ALU.mult, ALU.mult))
                    steps.wait()
                    steps.of(dve.tensor_tensor(tmp, tmp, var, ALU.mult))
                    steps.wait()
                    steps.of(dve.scalar_tensor_tensor(rstd, tmp, 1.5, rstd, ALU.add, ALU.mult))
                steps.wait()
                return dve.scalar_tensor_tensor(shift, mean, -1.0, rstd, ALU.mult, ALU.mult)

            def block_stats(q):
                for k in range(BLK):
                    steps.of(dve.bn_stats(st[:, bass.ds(BLK * q + k, 1), :].rearrange("p t c -> p (t c)"),
                                          xr[:, bass.ds(BLK * q + k, 1), :].rearrange("p t c -> p (t c)")))

            def first_bits(values, n_rounds):
                for r in range(n_rounds):
                    steps.of(dve.max(top[:, 8 * r:8 * r + 8], values))
                    steps.wait()
                    if r < n_rounds - 1:
                        steps.of(dve.match_replace(values, top[:, 8 * r:8 * r + 8], values, 0.0))
                        steps.wait()

            class Do(Part):
                def setup(self):
                    for c in (a_key, reduced, x1_done, ev_ok[2], edge_ok[1], edge_ok[3], y_ok, x3_ok, x2_ok):
                        dve.sem_inc(c.sem, c.credit)
                    dve.memset(xr[:, :, :], 0.0).then_inc(zero_set, 1)
                    dve.wait_ge(w_ld, 16 * N_LOADS)
                    steps.of(dve.tensor_copy(bit_u[:, :], cst[:, C_BIT:C_BIT + WORD]))
                    steps.of(dve.tensor_scalar(bias[0:1, :], bias[0:1, :], -1.0, None, ALU.add))
                    scratch = gath[:, 1, 0, :]
                    dve.wait_ge(w_ev, 1)
                    for w, k, at, a, H in [(w1_s, k, C, 2, HEADS) for k in range(2)] + [(w1_s, k, C + HEADS, 3, HEADS) for k in range(2)] \
                            + [(w3_s, k, C, 4, 1) for k in range(2)] + [(w3_s, k, C + 1, 5, 1) for k in range(2)]:
                        steps.of(dve.tensor_tensor(scratch, w[:, k, 0:C], gath[:, 0, a, :], ALU.mult))
                        steps.wait()
                        steps.of(dve.tensor_reduce(w[:, k, at:at + H], scratch.rearrange("p (h f) -> p h f", h=H), AX, ALU.add))
                        steps.wait()
                    steps.end()
                    dve.sem_inc(w_done, 1)
                    dve.wait_ge(w_done, 1)

                def pre(self, u, n, part):
                    if part != 6:
                        return
                    for i in range(2):
                        dve.wait_ge(xa_ld[i], 16 * n + 16)
                        dve.wait_ge(a_relu.sem, a_relu.free(u + i, 2))
                        steps.of(dve.bn_stats(st_a[:, i, :], xa[:, i, :]))
                    steps.wait()
                    for i in range(2):
                        steps.of(dve.bn_aggr(mv_a[:, i, :], st_a[:, i, :]))
                    steps.wait()
                    deviation(mv_a[:, :, 0], mv_a[:, :, 1], rn_a[:, :, 0], rn_a[:, :, 1], tmp_a[:, :]).then_inc(a_ln.sem, 2)
                    steps.end()

                def slot_front(self, T, par, n, part):
                    if part == 4:
                        self.find_words(T)
                    if part == 5:
                        self.find_bits(T, par)

                def find_words(self, T):
                    dve.wait_ge(a_pack.sem, a_pack.ready(2 * T + 1))
                    steps.of(dve.scalar_tensor_tensor(key[:, :], words, 0.0, cst[:, C_BASE:C_BASE + NW], ALU.is_gt, ALU.mult))
                    steps.wait()
                    dve.tensor_tensor(key[:, :], key[:, :], words, ALU.add).then_inc(a_key.sem, 1)
                    dve.wait_ge(a_key.sem, a_key.ready(T))
                    steps.carry()
                    first_bits(key[:, :], 4)
                    steps.end()

                def find_bits(self, T, par):
                    steps.of(dve.tensor_copy(topu[:, :], top[:, 0:S]))
                    steps.wait()
                    steps.of(dve.tensor_scalar(hi8[:, :], topu[:, :], 8, 3, ALU.logical_shift_right, ALU.logical_shift_left))
                    steps.of(dve.tensor_tensor(bits[:, :, :], topu[:, :].unsqueeze(2).to_broadcast([P, S, WORD]),
                                               bit_u[:, :].unsqueeze(1).to_broadcast([P, S, WORD]), ALU.bitwise_and))
                    steps.wait()
                    steps.of(dve.tensor_tensor(score[:, :, :], hi8[:, :].unsqueeze(2).to_broadcast([P, S, WORD]),
                                               cst[:, C_R:C_R + WORD].unsqueeze(1).to_broadcast([P, S, WORD]), ALU.subtract))
                    steps.wait()
                    steps.of(dve.scalar_tensor_tensor(score[:, :, :], bits[:, :, :], 0.0, score[:, :, :], ALU.is_gt, ALU.mult))
                    steps.wait()
                    first_bits(key[:, 0:S * WORD], 4)
                    dve.tensor_scalar(idx[:, par, :], top[:, 0:S], -1.0, cst[:, bass.ds(T + C_OFF, 1)], ALU.mult, ALU.add)\
                       .then_inc(idx_ready.sem, 1)
                    dve.wait_ge(idx_ready.sem, idx_ready.ready(T))
                    steps.carry()
                    steps.end()

                def slot_back(self, T, par, n, part, front):
                    if part == 0:
                        dve.wait_ge(gathered[par], 16 * S * n + 16 * S)
                        dve.wait_ge(cat_tr.sem, cat_tr.free(T, 1))
                    if part < 4:
                        c0, c1 = part * C // 4, (part + 1) * C // 4
                        ins = dve.tensor_reduce(cat[:, C + c0:C + c1], gath[:, par, :, c0:c1].rearrange("p s c -> p c s"), AX, ALU.max)
                        if part == 3:
                            ins.then_inc(reduced.sem, 1)
                    if part == 7:
                        dve.wait_ge(o_done.sem, o_done.ready(T))
                        dve.wait_ge(x1_ld, 16 * T + 16)
                        dve.scalar_tensor_tensor(x1[:, :], o_mm, -1.0, x1[:, :], ALU.max, ALU.add).then_inc(x1_done.sem, 1)

                def prep(self, p, b, g, part):
                    G = NQ * b + g
                    if p == 2 and part == 2:
                        here = slice(BLK * g, BLK * g + BLK)
                        hi, mid, low = split[:, here, 2 * C:3 * C], split[:, here, 0:C], split[:, here, C:2 * C]
                        dve.wait_ge(hi_ok.sem, hi_ok.ready(G))
                        dve.wait_ge(ut_ok.sem, ut_ok.ready(G))
                        steps.of(dve.tensor_tensor(res, acc[:, :, 0:C], hi, ALU.subtract))
                        steps.wait()
                        steps.of(dve.tensor_copy(mid, res))
                        steps.wait()
                        steps.of(dve.tensor_tensor(res, res, mid, ALU.subtract))
                        steps.wait()
                        dve.tensor_copy(low, res).then_inc(ev_ok[2].sem, 1)
                        dve.wait_ge(ev_ok[2].sem, ev_ok[2].ready(G))
                        steps.carry()
                        steps.end()

                def norm(self, p, b):
                    if p == 1:
                        for g in range(NQ):
                            dve.wait_ge(xr_ld, 16 * NQ * b + 16 * g + 16)
                            block_stats(g)
                        steps.wait()
                    if p == 2:
                        steps.of(dve.memset(split[:, :, 3 * C:3 * C + 1], 1.0))
                    for t in range(NT):
                        steps.of(dve.bn_aggr(mv[:, t, :], st[:, t, :]))
                    steps.wait()
                    deviation(mv[:, :, 0], mv[:, :, 1], rs[:, :], nm[:, :], tmp[:, :]).then_inc(ln_ok[p].sem, 1)
                    steps.end()

                def spread(self, p, b):
                    H = heads(p)
                    dve.wait_ge(ev_ok[p].sem, ev_ok[p].ready(NQ * b + NQ - 1))
                    dve.tensor_reduce(dmx[:, 0:H], sd[:, :, H:2 * H].rearrange("p t h -> p h t"), AX, ALU.max).then_inc(gd[p], 1)
                    dve.wait_ge(gp[p], 2 * b + 1)
                    steps.of(dve.tensor_reduce(dtop[0:H, :], psB[0:H, 0:P], AX, ALU.max))
                    steps.wait()
                    dve.tensor_scalar(ddiag[0:H, 0:H], cst[0:H, C_ID:C_ID + H], dtop[0:H, :], None, ALU.mult).then_inc(gd[p], 1)
                    dve.wait_ge(gp[p], 2 * b + 2)
                    D = psB[:, P:P + H].unsqueeze(1).to_broadcast([P, NT, H])
                    steps.of(dve.tensor_tensor(dd[:, :, 0:H], sd[:, :, H:2 * H], D, ALU.subtract))
                    steps.of(dve.tensor_tensor(sp_[:, :, 0:H], sd[:, :, 0:H], D, ALU.add))
                    steps.wait()
                    steps.of(dve.tensor_scalar(sp_[:, :, 0:H], sp_[:, :, 0:H], LIM, None, ALU.min))
                    dve.tensor_scalar(dd[:, :, 0:H], dd[:, :, 0:H], -LIM, None, ALU.max).then_inc(gd[p], 1)
                    dve.wait_ge(ga[p], b + 1)
                    W = C // H + 1
                    vals = V[p].rearrange("p t (h f) -> p t h f", h=H)
                    if H == 1:
                        steps.of(dve.tensor_tensor(vals[:, :, 0, 0:C], vals[:, :, 0, 0:C], vv[:, :, 0:1].to_broadcast([P, NT, C]), ALU.mult))
                    else:
                        flat = region[:, 0:val_cols].rearrange("p (t f) -> p t f", f=W)
                        steps.of(dve.tensor_tensor(flat[:, :, 0:F], flat[:, :, 0:F],
                                                   vv[:, :, :].rearrange("p t h -> p (t h)").unsqueeze(2).to_broadcast([P, NT * H, F]), ALU.mult))
                    steps.of(dve.tensor_copy(vals[:, :, :, W - 1], vv[:, :, 0:H]))
                    steps.end()
                    dve.sem_inc(gd[p], 1)

                def attend_start(self, p, b, q):
                    if p == 3:
                        dve.tensor_copy(sq[:, :], sp_[:, bass.ds(BLK * q, BLK), 0]).then_inc(sq_ok.sem, 1)

                def attend(self, p, b, q, J):
                    H, Q = heads(p), NQ * b + q
                    for h in range(H):
                        n = H * J + h
                        if J == 0:
                            dve.wait_ge(wB_ok[p].sem, wB_ok[p].ready(H * Q + h))
                        dve.wait_ge(mm_ok[p].sem, mm_ok[p].free(NT * H * Q + n, 4))
                        dve.scalar_tensor_tensor(
                            edge[:, n % 4, :], wB[:, h, :], gg[:, J, h:h + 1],
                            adjT[:, J, bass.ds((b % 2) * N + 512 * q, 512)], ALU.max, ALU.mult).then_inc(edge_ok[p].sem, 1)

                def result(self, b, q, k):
                    y, e = result_of(q, k)
                    n = BLK * (NQ * b + q) + k
                    dve.wait_ge(back_ok.sem, back_ok.ready(n))
                    sums = psB[:, 0:HEADS * (F + 1)].rearrange("p (h f) -> p h f", h=HEADS)
                    steps.of(dve.reciprocal(den[:, k, :], sums[:, :, F]))
                    steps.wait()
                    dve.tensor_tensor(y.rearrange("p (h f) -> p h f", h=HEADS), sums[:, :, 0:F],
                                      den[:, k, :].unsqueeze(2).to_broadcast([P, HEADS, F]), ALU.mult).then_inc(y_ok.sem, 1)
                    steps.end()

                def add(self, b, q, k):
                    y, e = result_of(q, k)
                    t, n = BLK * q + k, BLK * (NQ * b + q) + k
                    dve.wait_ge(e_ok.sem, e_ok.ready(n))
                    steps.of(dve.scalar_tensor_tensor(e, e, 1.0, xr[:, t, :], ALU.min, ALU.add))
                    steps.wait()
                    steps.of(dve.scalar_tensor_tensor(xr[:, t, :], y, 0.0, e, ALU.max, ALU.add))
                    steps.wait()
                    steps.of(dve.bn_stats(st[:, t, :], xr[:, t, :]))
                    steps.end()

                def attend_end(self, p, b, q):
                    if p == 1:
                        return
                    Q = NQ * b + q
                    dve.wait_ge(mm_ok[3].sem, mm_ok[3].ready(NT * Q + NT - 1))
                    steps.of(dve.reciprocal(den[:, :, 0:1], acc[:, :, C:C + 1]))
                    steps.wait()
                    for k in range(BLK):
                        row = xr[:, bass.ds(BLK * q + k, 1), :].rearrange("p t c -> p (t c)")
                        ins = dve.scalar_tensor_tensor(row, acc[:, k, 0:C], den[:, k, 0:1], row, ALU.mult, ALU.add)
                    ins.then_inc(x3_ok.sem, 1)
                    steps.end()

                def mean(self, b, q, k, m):
                    if m == 1 and k > 0:
                        self.finish(b, q, k - 1)
                    if m == 3 and k == BLK - 1:
                        self.finish(b, q, k)

                def finish(self, b, q, k):
                    J = 4 * (NQ * b + q) + k
                    if k == 0:
                        dve.wait_ge(u_ld, 16 * (NQ * b + q) + 16)
                    dve.wait_ge(c_mm.sem, c_mm.ready(4 * J + 3))
                    steps.of(dve.tensor_scalar(den[:, k, 0:1], acc[:, k, C:C + 1], 1.0, None, ALU.max))
                    steps.wait()
                    steps.of(dve.reciprocal(den[:, k, 1:2], den[:, k, 0:1]))
                    steps.wait()
                    steps.of(dve.scalar_tensor_tensor(res[:, k, :], acc[:, k, 0:C], den[:, k, 1:2], u2_s[:, k, :], ALU.mult, ALU.add))
                    steps.wait()
                    row = xr[:, bass.ds(BLK * q + k, 1), :].rearrange("p t c -> p (t c)")
                    dve.scalar_tensor_tensor(row, res[:, k, :], 0.0, row, ALU.max, ALU.add).then_inc(x2_ok.sem, 1)
                    dve.wait_ge(x2_ok.sem, x2_ok.ready(J))
                    if k == BLK - 1:
                        block_stats(q)
                    else:
                        steps.carry()
                    steps.end()

            program(dve, Do())


N_LOADS = 11
_INS = ["x", "adj", "L0_gnn_W", "L0_gnn_b", "L1_gnn_W", "L1_gnn_a_src", "L1_gnn_a_dst", "L2_gnn_W_msg", "L2_gnn_W_upd",
        "L2_gnn_bias", "L3_gnn_W", "L3_gnn_a"]


def kernel(**inputs):
    import numpy as np
    import concourse.bacc as bacc
    from concourse.bass_utils import run_bass_kernel_spmd

    nc = bacc.Bacc("TRN2", target_bir_lowering=False, num_devices=1)
    arrays = {f"in_{n}": np.ascontiguousarray(inputs[n]) for n in _INS}
    arrays["in_const"] = constants()
    args = [nc.dram_tensor(n, a.shape, mybir.dt.from_np(a.dtype), kind="ExternalInput").ap() for n, a in arrays.items()]
    out = nc.dram_tensor("out_0", (B, N, C), F32, kind="ExternalOutput").ap()
    gnn_kernel(nc, *args, out)
    r = run_bass_kernel_spmd(nc, [arrays], core_ids=[0])
    return r.results[0]["out_0"]
```

```python
from contextlib import ExitStack

import concourse.bass as bass
from concourse import mybir

F32 = mybir.dt.float32
BF16 = mybir.dt.bfloat16
I32 = mybir.dt.int32
U32 = mybir.dt.uint32
U8 = mybir.dt.uint8
ALU = mybir.AluOpType
ACT = mybir.ActivationFunctionType
AX = mybir.AxisListType.X

P = 128
B = 8
N = 2048
C = 256
NT = N // P
BLK = 4
NQ = NT // BLK
S = 25
HEADS = 4
F = C // HEADS
WORD = 8
NW = N // WORD
WPT = P // WORD
TAB = N + 1
SLOTS = NT
LAG = 2
EPS = 1e-5
SLOPE = 0.2
LIM = 90.0

C_ID, C_BASE, C_OFF = 0, P, P + NW
C_PACK = C_OFF + B * NT
C_R = C_PACK + WPT
C_BIT = C_R + WORD
C_ONE = C_BIT + WORD
C_END = C_ONE + 1


def constants():
    import numpy as np
    c = np.zeros((P, C_END), np.float32)
    p = np.arange(P)
    c[:, C_ID:C_ID + P] = np.eye(P)
    c[:, C_ONE] = 1.0
    c[:, C_BASE:C_BASE + NW] = (NW - np.arange(NW)) * 256.0
    c[:, C_OFF:C_OFF + B * NT] = N + TAB * (np.arange(B * NT) // NT % 2)
    c[p, C_PACK + p // WORD] = 2.0 ** (WORD - 1 - p % WORD)
    c[:, C_R:C_R + WORD] = np.arange(WORD)
    c[:, C_BIT:C_BIT + WORD] = 2.0 ** (WORD - 1 - np.arange(WORD))
    return c


class Count:

    def __init__(self, sem, credit=0):
        self.sem, self.credit = sem, credit

    def ready(self, n):
        return n + (self.credit + 1)

    def free(self, n, depth):
        assert self.credit >= depth
        return n + (self.credit + 1 - depth)


def gnn_kernel(nc, x, adj, w0, b0, w1, a1s, a1d, w2m, w2u, b2, w3, a3, const, out):
    ctx = ExitStack()
    with ctx:
        def sb(name, shape, dt):
            return ctx.enter_context(nc.sbuf_tensor(name, shape, dt))

        def sem(name):
            return ctx.enter_context(nc.semaphore(name))

        def count(name, credit=0):
            return Count(sem(name), credit)

        htab = nc.dram_tensor("htab", [2 * TAB, C], F32, kind="Internal").ap()
        x1d = nc.dram_tensor("x1d", [B * N, C], F32, kind="Internal").ap()
        u2d = nc.dram_tensor("u2d", [N, C], F32, kind="Internal").ap()
        rows = lambda t: t.rearrange("(t p) c -> p t c", p=P)
        x_r, x1_r, u2_r = rows(x.rearrange("b n c -> (b n) c")), rows(x1d), rows(u2d)
        out_r = rows(out.rearrange("b n c -> (b n) c"))
        adj_r = adj.rearrange("b (i p) j -> p (b i) j", p=P)

        cst = sb("cst", [P, C_END], F32)
        ident, one = cst[:, C_ID:C_ID + P], cst[:, C_ONE:C_ONE + 1]
        ident_bf = sb("ident_bf", [P, P], BF16)
        pack_bf = sb("pack_bf", [P, WPT], BF16)
        bit_u = sb("bit_u", [P, WORD], U32)
        w0_s = sb("w0_s", [P, 4, C], F32)
        w1_s = sb("w1_s", [P, 2, C + 2 * HEADS], F32)
        w2_s = sb("w2_s", [P, 2, 2 * C], F32)
        w3_s = sb("w3_s", [P, 2, C + 2], F32)
        bias = sb("bias", [P // 4 + 1, C], F32)
        adj_i = sb("adj_i", [P, 2, 512], I32)
        adj_b = sb("adj_b", [P, 2, 512], BF16)
        adjT_b = sb("adjT_b", [P, 1024], BF16)
        adjT = sb("adjT", [P, NT, 2 * N], U8)
        key = sb("key", [P, NW], F32)
        top = sb("top", [P, 32], F32)
        topu = sb("topu", [P, S], U32)
        hi8 = sb("hi8", [P, S], U32)
        bits = sb("bits", [P, S, WORD], U32)
        score = key[:, 0:S * WORD].rearrange("p (s r) -> p s r", s=S)
        idx = sb("idx", [P, 2, S], U32)
        gath = sb("gath", [P, 2, S, C], F32)
        cat = sb("cat", [P, 2 * C], F32)
        catT = sb("catT", [P, 4, P], F32)
        x1 = sb("x1", [P, C], F32)
        xa = sb("xa", [P, 2, C], F32)
        st_a = sb("st_a", [P, 2, 6], F32)
        mv_a = sb("mv_a", [P, 2, 2], F32)
        rn_a = sb("rn_a", [P, 2, 2], F32)
        xr = sb("xr", [P, NT, C], F32)
        hb = sb("hb", [P, BLK, C], F32)
        st = sb("st", [P, NT, 6], F32)
        mv = sb("mv", [P, NT, 2], F32)
        rs = sb("rs", [P, NT], F32)
        nm = sb("nm", [P, NT], F32)
        tmp = sb("tmp", [P, NT], F32)
        tmp_a = sb("tmp_a", [P, 2], F32)
        sd = sb("sd", [P, NT, 2 * HEADS], F32)
        dmx = sb("dmx", [P, HEADS], F32)
        dtop = sb("dtop", [HEADS, 1], F32)
        ddiag = sb("ddiag", [HEADS, HEADS], F32)
        dd = sb("dd", [P, NT, HEADS], F32)
        sp_ = sb("sp_", [P, NT, HEADS], F32)
        vv = sb("vv", [P, NT, HEADS], F32)
        gg = sb("gg", [P, NT, HEADS], F32)
        den = sb("den", [P, BLK, HEADS], F32)
        col_i = sb("col_i", [P, 2, 4, P], I32)
        hb_f = hb[:, :, :].rearrange("p a c -> p (a c)")
        col_f = col_i[:, :, :, :].rearrange("p m i j -> p (m i j)").bitcast(F32)
        hb_i = hb_f.bitcast(I32).rearrange("p (m i j) -> p m i j", m=2, i=4)
        cols = [hb_i[:, 0, :, :], hb_i[:, 1, :, :], col_i[:, 0, :, :], col_i[:, 1, :, :]]
        col_b = sb("col_b", [P, 2, 4, P], BF16)
        ye = col_b[:, :, :, :].rearrange("p m i j -> p (m i j)").bitcast(F32)
        val_cols = NT * HEADS * (F + 1)
        region = sb("region", [P, val_cols + HEADS * 512], F32)
        V = {1: region[:, 0:val_cols].rearrange("p (t c) -> p t c", t=NT),
             3: region[:, 0:NT * (C + 1)].rearrange("p (t c) -> p t c", t=NT)}
        wB = region[:, val_cols:val_cols + HEADS * 512].rearrange("p (h i) -> p h i", h=HEADS)
        SPL = 3 * C + 2
        split = region[:, 0:NT * SPL // 2].bitcast(BF16).rearrange("p (t c) -> p t c", t=NT)
        h0 = region[:, 0:NT * C].rearrange("p (t c) -> p t c", t=NT)
        edge = sb("edge", [P, 4, 512], F32)
        edge_f = edge[:, :, :].rearrange("p a c -> p (a c)")
        hT = [edge_f[:, 512 * i:512 * i + 512].rearrange("p (t k r) -> p t k r", t=2, k=2) for i in range(2)]
        res = [edge_f[:, 1024 + 512 * i:1536 + 512 * i].rearrange("p (t c) -> p t c", t=2) for i in range(2)]
        u2_s = edge_f[:, 0:1024].rearrange("p (t c) -> p t c", t=BLK)

        u_s = [col_f[:, 512 * i:512 * i + 512].rearrange("p (t c) -> p t c", t=2) for i in range(2)]
        cols_b = [col_b[:, 0, :, :], col_b[:, 1, :, :]] + \
            [edge_f[:, 1280 + 256 * i:1536 + 256 * i].bitcast(BF16).rearrange("p (i j) -> p i j", i=4) for i in range(2)]
        yT = [hb_f[0:F + 1, 0:512], hb_f[0:F + 1, 512:1024], col_f[0:F + 1, 0:512], col_f[0:F + 1, 512:1024]]

        def result_of(q, k):
            if q == NQ - 1:
                wB_f = region[:, val_cols:val_cols + 2 * BLK * C]
                return wB_f[:, C * k:C * k + C], wB_f[:, C * (BLK + k):C * (BLK + k) + C]
            return ye[:, 0:C], ye[:, C:2 * C]

        def pb(name, shape, dt):
            return ctx.enter_context(nc.psum_tensor(name, shape, dt))

        acc = pb("acc", [P, BLK, 512], F32)
        psT = pb("psT", [P, 1024], BF16)
        psH = pb("psH", [P, 512], F32)
        psO = pb("psO", [P, 512], F32)
        psB = pb("psB", [P, 512], F32)
        o_mm, words = psH[:, 0:C], psO[:, 0:NW]

        w_ld, w_cast, w_red, w_tr, w_ev, w_done = (sem(n) for n in ("w_ld", "w_cast", "w_red", "w_tr", "w_ev", "w_done"))
        tiles_begun, loads_begun = sem("tiles_begun"), sem("loads_begun")
        zero_st, zero_set = sem("zero_st"), sem("zero_set")
        x0_ld, ln0_ok, h0_ok = [sem("x0_ld0"), sem("x0_ld1")], sem("ln0_ok"), sem("h0_ok")
        chain = sem("chain")
        a_ld = [sem("a_ld0"), sem("a_ld1")]
        a_cast, a_used = count("a_cast", 2), count("a_used", 2)
        a_evac, a_copied, a_pack = count("a_evac", 1), count("a_copied", 1), count("a_pack", 1)
        a_key, idx_ready, reduced = count("a_key", 1), count("idx_ready"), count("reduced", 2)
        gathered = [sem("gathered0"), sem("gathered1")]
        xa_ld = [sem("xa_ld0"), sem("xa_ld1")]
        a_ln, a_relu = count("a_ln"), count("a_relu", 2)
        h_dma, x1_dma = sem("h_dma"), sem("x1_dma")
        cat_ld, x1_ld = sem("cat_ld"), sem("x1_ld")
        cat_tr, cat_ev, o_done, x1_done = (count(n, m) for n, m in (("cat_tr", 1), ("cat_ev", 1), ("o_done", 1), ("x1_done", 3)))
        xr_ld = [sem("xr_ld0"), sem("xr_ld1")]
        ln_ok = {p: count(f"ln{p}") for p in (1, 2, 3)}
        h_ok = {p: count(f"h{p}", 2) for p in (1, 2, 3)}
        tp_ok = {p: count(f"tp{p}", 2) for p in (1, 2, 3)}
        hT_ok = {p: count(f"hT{p}", 1) for p in (1, 2, 3)}
        dn_ok = {p: count(f"dn{p}", 2) for p in (1, 2, 3)}
        ev_ok = {p: count(f"ev{p}", 2) for p in (1, 2, 3)}
        hi_ok, ut_ok, u_dma, u_stored = count("hi_ok"), count("ut_ok"), sem("u_dma"), count("u_stored", 2)
        gd = {p: sem(f"gd{p}") for p in (1, 3)}
        gp = {p: sem(f"gp{p}") for p in (1, 3)}
        ga = {p: sem(f"ga{p}") for p in (1, 3)}
        sB_ok = {p: count(f"sB{p}") for p in (1, 3)}
        wB_ok = {p: count(f"wB{p}", 1) for p in (1, 3)}
        edge_ok = {p: count(f"edge{p}", 4) for p in (1, 3)}
        mm_ok = {p: count(f"mm{p}", 4) for p in (1, 3)}
        x3_ok = count("x3_ok", 1)
        yT_ok, back_ok, y_ok, e_ok = count("yT_ok", 4), count("back_ok"), count("y_ok", 1), count("e_ok")
        out_st = sem("out_st")
        c_ld = [sem(f"c_ld{m}") for m in range(4)]
        c_cast, c_mm, x2_ok, u_ld = count("c_cast", 4), count("c_mm", 4), count("x2_ok", 4), sem("u_ld")

        def front_tile(b, sh, par):
            return 16 * (b + 1) + LAG + 2 * sh + par

        def back_tile(b, sh, par):
            return 16 * (b + 1) + 2 * sh + par

        def half(b, sh):
            return 8 * (b + 1) + sh

        PARTS = 16
        GROUPS = NT // 2
        PLAN = [("prep1", 1), ("attend1", 1), ("prep2", 1), ("mean", 2), ("prep3", 1), ("attend3", 2)]
        assert 2 * sum(n for _, n in PLAN) == SLOTS

        def body(eng, b, do, front=lambda s: True, pre=True, slots=True):
            def steps_of(phase, q, odd):
                if phase.startswith("prep"):
                    p = int(phase[-1])
                    steps = [lambda n=n, part=part: do.prep(p, b, n, part) for n in (2 * q, 2 * q + 1) for part in range(2)]
                    if q == 0:
                        steps.insert(2 if p == 1 else 1, lambda: do.norm(p, b, 1))
                    return steps
                if phase == "mean":
                    return [lambda k=k, m=m: do.mean(b, q, k, m, odd) for k in range(BLK) for m in range(4)]
                p = int(phase[-1])
                steps = [lambda J=J: do.attend(p, b, q, J) for J in range(NT)]
                if p == 3:
                    if q == 0:
                        steps.insert(0, lambda: do.attend_start(3, b, 0))
                    else:
                        steps.insert(1, lambda: do.attend_end(3, b, q - 1))
                    if q == NQ - 1:
                        if slots:
                            steps.insert(12, lambda: do.norm(1, b + 1, 0))
                        steps.append(lambda: do.attend_end(3, b, q))
                    if slots and q > 1:
                        steps.insert(3, lambda: do.fetch(b + 1, q - 2))
                    if slots and q == NQ - 1:
                        steps.insert(6, lambda: do.fetch(b + 1, q - 1))
                    return steps
                if q == 0:
                    return [lambda: do.attend_start(1, b, 0)] + steps + [lambda: do.attend_end(1, b, 0)]
                taken = []
                for k in range(BLK):
                    J = (1, 4, 8, 12)[k]
                    for at, f in ((J, do.turn_back), (J + 2, do.result), (J + 3, do.add)):
                        steps.insert(at + sum(n <= at for n in taken), lambda f=f, k=k: f(b, q - 1, k))
                        taken.append(at)
                steps.append(lambda: do.attend_end(1, b, q))
                if q == NQ // 2:
                    steps.append(lambda: do.norm(2, b, 0))
                if q == NQ - 1:
                    tail = [(do.turn_back, 0), (do.result, 0)]
                    for k in range(1, BLK):
                        tail += [(do.turn_back, k), (do.result, k), (do.add, k - 1)]
                    tail.append((do.add, BLK - 1))
                    steps += [lambda f=f, k=k: f(b, q, k) for f, k in tail]
                return steps

            def pair(phase, r, n, s0, pre_0):
                main = steps_of(phase, 2 * r, False) + steps_of(phase, 2 * r + 1, True)
                side = []
                for i in range(n if slots else 0):
                    sh, par = s0(i)
                    k = None if pre_0 is None or not pre else pre_0 + i
                    side += [lambda part=part, sh=sh, par=par, k=k: do.slot(b, sh, par, part, front, k) for part in range(PARTS)]
                done = 0
                lead, rest = (2, 0) if phase.startswith("attend") and r == 0 else (0, 2) if phase.startswith("prep") else (0, 0)
                for i, step in enumerate(main):
                    while done * (len(main) - lead - rest) < (i + 1 - lead) * len(side) and done < len(side):
                        side[done]()
                        done += 1
                    step()

            s = pre_done = 0
            for phase, n in PLAN:
                if phase.startswith("prep"):
                    p = int(phase[-1])
                    if p == 3:
                        do.norm(3, b, 0)
                    do.prep_start(p, b)
                early = phase not in ("mean", "attend3")
                if phase == "mean":
                    with eng.Fori(0, NQ // 2) as r:
                        pair(phase, r, n, lambda i: (r * (n // 2) + (s + i) // 2, i % 2), None)
                else:
                    for r in range(NQ // 2):
                        pair(phase, r, n, lambda i: ((s + n * r + i) // 2, (s + n * r + i) % 2), pre_done + n * r if early else None)
                pre_done += 2 * n if early else 0
                s += 2 * n
                if phase in ("prep1", "prep3"):
                    do.spread(int(phase[-1]), b)
            assert pre_done == NT // 2
            if slots:
                do.fetch(b + 1, NQ - 1)
            do.end(b)

        def program(eng, do):
            do.setup()
            do.first_h()
            for part in range(PARTS):
                do.ahead(0, part)
            for T in range(LAG):
                for part in range(PARTS):
                    do.slot_front(T, T, 0, part)
                    do.ahead(T + 1, part)
            for first in (0, 4):
                with eng.Fori(first, first + 4) as sh:
                    for par in range(2):
                        for part in range(PARTS):
                            do.slot(-1, sh, par, part, lambda s: True, 2 * sh + par if first == 0 else None)
            for g in range(NQ):
                do.fetch(0, g)
            do.norm(1, 0, 0)
            with eng.Fori(0, B - 2) as b:
                body(eng, b, do)
            body(eng, B - 2, do, front=lambda s: s < SLOTS - LAG, pre=False)
            body(eng, B - 1, do, slots=False)

        class Part:
            def setup(self): pass
            def first_h(self): pass
            def pre(self, u, n, part): pass
            def slot_front(self, T, par, n, part): pass
            def slot_back(self, T, par, n, part, front): pass
            def prep_start(self, p, b): pass
            def prep(self, p, b, n, part): pass
            def spread(self, p, b): pass
            def attend_start(self, p, b, q): pass
            def attend(self, p, b, q, J): pass
            def attend_end(self, p, b, q): pass
            def turn_back(self, b, q, k): pass
            def result(self, b, q, k): pass
            def add(self, b, q, k): pass
            def fetch(self, b, g): pass
            def norm(self, p, b, half): pass
            def ahead(self, T, part): pass
            def mean(self, b, q, k, m, odd): pass
            def end(self, b): pass

            def slot(self, b, sh, par, part, front, k):
                known = isinstance(sh, int)
                enters = not known or front(2 * sh + par)
                next_enters = not known or front(2 * sh + par + 1)
                Tf, Tb, n = front_tile(b, sh, par), back_tile(b, sh, par), half(b, sh)
                if part == 0:
                    self.slot_back(Tb, par, n, part, enters)
                if enters:
                    self.slot_front(Tf, par, n + LAG // 2, part)
                if k is not None:
                    self.pre(16 * (b + 2) + 2 * k, 8 * (b + 2) + k, part)
                if part != 0:
                    self.slot_back(Tb, par, n, part, enters)
                if next_enters:
                    self.ahead(Tf + 1, part)

        def table_row(T):
            return (T % (2 * NT)) * P + (T % (2 * NT)) // NT

        def heads(p):
            return HEADS if p == 1 else 1

        block = ctx.enter_context(nc.Block())

        @block.sync
        def _(sp):
            class Do(Part):
                def setup(self):
                    sp.sem_inc(u_stored.sem, u_stored.credit)
                    for credit in (x1_dma, xr_ld[0], xr_ld[1]):
                        sp.sem_inc(credit, 16)
                    for g in range(NQ):
                        if g > 1:
                            sp.wait_ge(x0_ld[g % 2], 16)
                        sp.dma_start(xr[:, BLK * g:BLK * g + BLK, :], x_r[:, BLK * g:BLK * g + BLK, :]).then_inc(x0_ld[g % 2], 16)
                    kp = "(k p) n -> p k n"
                    tmp = gath[:, 0, :, :]
                    loads = [
                        (cst[:, :], const), (w0_s[:, :, :], w0.rearrange(kp, p=P)),
                        (w1_s[:, :, 0:C], w1.rearrange(kp, p=P)),
                        (w2_s[:, :, 0:C], w2m.rearrange(kp, p=P)), (w2_s[:, :, C:2 * C], w2u.rearrange(kp, p=P)),
                        (tmp[:, 0:2, :], w3.rearrange(kp, p=P)),
                        (tmp[:, 2, :], a1s.rearrange("h f -> (h f)").partition_broadcast(P)),
                        (tmp[:, 3, :], a1d.rearrange("h f -> (h f)").partition_broadcast(P)),
                        (tmp[:, 4:6, :], a3.rearrange("a (k c) -> (a k) c", k=2).partition_broadcast(P)),
                        (bias[0:1, :], b0.rearrange("(a c) -> a c", a=1)),
                        (bias[32:33, :], b2.rearrange("(a c) -> a c", a=1)),
                    ]
                    assert len(loads) == N_LOADS
                    for to, fr in loads:
                        sp.dma_start(to, fr).then_inc(w_ld, 16)
                    zeros = gath[:, 1, 0:NT, :]
                    sp.wait_ge(zero_set, 1)
                    sp.dma_start(htab[N + 1:2 * N + 1, :].rearrange("(p t) c -> p (t c)", p=P), zeros.rearrange("p t c -> p (t c)")).then_inc(zero_st, 16)
                    sp.dma_start(htab[N:N + 1, :], zeros[0:1, 0, :]).then_inc(zero_st, 16)
                    sp.dma_start(htab[2 * N + 1:2 * TAB, :], zeros[0:1, 0, :]).then_inc(zero_st, 16)
                    sp.wait_ge(zero_st, 48)

                def first_h(self):
                    for g in range(NQ):
                        sp.wait_ge(h0_ok, g + 1)
                        sp.dma_start(htab[P * BLK * g:P * BLK * (g + 1), :].rearrange("(t p) c -> p t c", p=P),
                                     h0[:, BLK * g:BLK * g + BLK, :]).then_inc(h_dma, 16)
                    sp.wait_ge(h_dma, 16 * NQ)
                    sp.sem_inc(h_dma, 16 * (NT + 1 - NQ))

                def pre(self, u, n, part):
                    if part == 0:
                        sp.wait_ge(h_dma, 16 * u + 16)
                        for i in range(2):
                            sp.dma_start(xa[:, i, :], x_r[:, bass.ds(u + i, 1), :].rearrange("p t c -> p (t c)")).then_inc(xa_ld[i], 16)
                    if part == 14:
                        for i in range(2):
                            sp.wait_ge(a_relu.sem, a_relu.ready(u + i))
                            sp.dma_start(htab[bass.ds(table_row(u + i), P), :], xa[:, i, :]).then_inc(h_dma, 16)

                def slot_back(self, T, par, n, part, front):
                    if part == 0:
                        sp.wait_ge(cat_tr.sem, cat_tr.free(T, 1))
                        sp.wait_ge(h_dma, (T // NT) * (16 * NT) + 16 * NT + 16)
                        sp.dma_start(cat[:, 0:C], htab[bass.ds(table_row(T), P), :]).then_inc(cat_ld, 16)
                    if part == 2:
                        sp.wait_ge(x1_dma, 16 * T + 16)
                        sp.dma_start(x1[:, :], x_r[:, bass.ds(T, 1), :].rearrange("p t c -> p (t c)")).then_inc(x1_ld, 16)
                    if part == 15:
                        sp.wait_ge(x1_done.sem, x1_done.ready(T))
                        sp.dma_start(x1_r[:, bass.ds(T, 1), :].rearrange("p t c -> p (t c)"), x1[:, :]).then_inc(x1_dma, 16)

                def fetch(self, b, g):
                    if not isinstance(b, int) or b > 0:
                        sp.wait_ge(out_st, 16 * (NQ * (b - 1) + g + 1))
                    sp.wait_ge(x1_dma, 16 * (NT * b + BLK * g + BLK) + 16)
                    sp.wait_ge(xr_ld[g % 2], 16 * (2 * b + g // 2) + 16)
                    sp.dma_start(xr[:, BLK * g:BLK * g + BLK, :], x1_r[:, bass.ds(NT * b + BLK * g, BLK), :]).then_inc(xr_ld[g % 2], 16)

                def prep(self, p, b, n, part):
                    G = GROUPS * b + n
                    if p == 2 and part == 1:
                        sp.wait_ge(ut_ok.sem, ut_ok.ready(G))
                        sp.dma_start(u2_r[:, 2 * n:2 * n + 2, :], u_s[n % 2]).then_inc(u_dma, 16)
                        sp.wait_ge(u_dma, 16 * G + 16)
                        sp.sem_inc(u_stored.sem, 1)

                def mean(self, b, q, k, m, odd):
                    if k == 0 and m == 2:
                        sp.wait_ge(ev_ok[2].sem, ev_ok[2].ready(GROUPS * b + GROUPS - 1))
                        sp.wait_ge(x2_ok.sem, x2_ok.free(4 * (NQ * b + q) + 3, 4))
                        sp.dma_start(u2_s, u2_r[:, bass.ds(BLK * q, BLK), :]).then_inc(u_ld, 16)

                def attend_end(self, p, b, q):
                    if p == 3:
                        Q = NQ * b + q
                        sp.wait_ge(x3_ok.sem, x3_ok.ready(Q))
                        sp.dma_start(out_r[:, bass.ds(BLK * Q, BLK), :], xr[:, bass.ds(BLK * q, BLK), :]).then_inc(out_st, 16)

                def end(self, b):
                    if isinstance(b, int) and b == B - 1:
                        sp.wait_ge(out_st, 16 * NQ * B)

            program(sp, Do())

        @block.gpsimd
        def _(pool):
            class Do(Part):
                def slot_front(self, T, par, n, part):
                    if part != 15:
                        return
                    pool.wait_ge(h_dma, (T // NT) * (16 * NT) + 16 * NT + 16)
                    pool.wait_ge(reduced.sem, reduced.free(T, 2))
                    pool.wait_ge(idx_ready.sem, idx_ready.ready(T))
                    pool.sem_inc(tiles_begun, 1)
                    for s in range(S):
                        pool.indirect_dma_start(
                            out=gath[:, par, s, :], out_offset=None, in_=htab,
                            in_offset=bass.IndirectOffsetOnAxis(ap=idx[:, par, s:s + 1], axis=0),
                        ).then_inc(gathered[par], 16)

            program(pool, Do())

        @block.scalar
        def _(act):
            class Do(Part):
                def setup(self):
                    for c in (a_cast, a_evac, a_copied, a_relu, cat_ev, h_ok[1], h_ok[2], h_ok[3], hT_ok[1], hT_ok[2], hT_ok[3], ev_ok[1], ev_ok[3], wB_ok[1], wB_ok[3], yT_ok, c_cast):
                        act.sem_inc(c.sem, c.credit)
                    act.sem_inc(a_relu.sem, NT)
                    act.wait_ge(w_ld, 16 * N_LOADS)
                    act.activation(ident_bf[:, :], ident, ACT.Copy).then_inc(w_cast, 1)
                    act.activation(pack_bf[:, :], cst[:, C_PACK:C_PACK + WPT], ACT.Copy).then_inc(w_cast, 1)
                    act.wait_ge(w_tr, 1)
                    act.activation(w3_s[:, :, 0:C], psH[:, :].rearrange("p (k o) -> p k o", k=2), ACT.Copy).then_inc(w_ev, 1)

                def first_h(self):
                    act.wait_ge(ln0_ok, 1)
                    for t in range(NT):
                        ins = act.activation(h0[:, t, :], xr[:, t, :], ACT.Relu, bias=nm[:, t:t + 1], scale=rs[:, t:t + 1])
                        if t % BLK == BLK - 1:
                            ins.then_inc(h0_ok, 1)

                def pre(self, u, n, part):
                    if part == 10:
                        for i in range(2):
                            act.wait_ge(a_ln.sem, a_ln.ready(u + i))
                            act.activation(xa[:, i, :], xa[:, i, :], ACT.Relu, bias=rn_a[:, i, 1:2], scale=rn_a[:, i, 0:1]).then_inc(a_relu.sem, 1)

                def slot_front(self, T, par, n, part):
                    def evacuate(half):
                        act.wait_ge(a_used.sem, a_used.ready(4 * T + 2 * half + 1))
                        act.wait_ge(a_pack.sem, a_pack.free(2 * T + half, 1))
                        act.activation(adjT_b[:, :], psT[:, :], ACT.Copy).then_inc(a_evac.sem, 1)

                    def keep(half):
                        act.activation(adjT[:, 8 * half:8 * half + 8, bass.ds((T % (2 * NT)) * P, P)],
                                       psT[:, :].rearrange("p (j i) -> p j i", j=8), ACT.Copy).then_inc(a_copied.sem, 1)

                    if part == 0:
                        self.load(T, 2)
                    if part in (2, 6):
                        evacuate((2, 6).index(part))
                    if part in (3, 4):
                        self.cast(T, part - 1)
                    if part in (3, 7):
                        keep((3, 7).index(part))

                def cast(self, T, k):
                    act.wait_ge(a_ld[k % 2], 32 * T + 16 * (k // 2) + 16)
                    act.wait_ge(a_used.sem, a_used.free(4 * T + k, 2))
                    act.activation(adj_b[:, k % 2, :], adj_i[:, k % 2, :], ACT.Copy).then_inc(a_cast.sem, 1)

                def load(self, T, first):
                    for k in range(first, first + 2):
                        act.wait_ge(a_cast.sem, a_cast.free(4 * T + k, 2))
                        act.dma_start(adj_i[:, k % 2, :], adj_r[:, bass.ds(T, 1), 512 * k:512 * k + 512].rearrange("p t c -> p (t c)")).then_inc(a_ld[k % 2], 16)

                def ahead(self, T, part):
                    if part == 8:
                        self.load(T, 0)
                    if part in (14, 15):
                        self.cast(T, part - 14)

                def slot_back(self, T, par, n, part, front):
                    if part == 9:
                        act.wait_ge(cat_tr.sem, cat_tr.ready(T))
                        act.wait_ge(o_done.sem, o_done.free(T, 1))
                        act.activation(catT[:, :, :].rearrange("p k r -> p (k r)"), psH[:, :], ACT.Copy).then_inc(cat_ev.sem, 1)

                def relu(self, p, b, n):
                    G = GROUPS * b + n
                    act.wait_ge(ln_ok[p].sem, ln_ok[p].ready(2 * b + 2 * n // GROUPS))
                    act.wait_ge(tp_ok[p].sem, tp_ok[p].free(G, 2))
                    for t in range(2 * n, 2 * n + 2):
                        ins = act.activation(hb[:, t % BLK, :], xr[:, t, :], ACT.Relu, bias=nm[:, t:t + 1], scale=rs[:, t:t + 1])
                    ins.then_inc(h_ok[p].sem, 1)

                def keep_hT(self, p, b, n):
                    G = GROUPS * b + n
                    act.wait_ge(tp_ok[p].sem, tp_ok[p].ready(G))
                    act.wait_ge(dn_ok[p].sem, dn_ok[p].free(G, 2))
                    act.activation(hT[n % 2].rearrange("p t k r -> p (t k r)"), psB[:, :], ACT.Copy).then_inc(hT_ok[p].sem, 1)

                def prep_start(self, p, b):
                    self.relu(p, b, 0)
                    self.relu(p, b, 1)
                    self.keep_hT(p, b, 0)

                def prep(self, p, b, n, part):
                    G = GROUPS * b + n
                    if part == 0:
                        if n < GROUPS - 2:
                            self.relu(p, b, n + 2)
                        if n < GROUPS - 1:
                            self.keep_hT(p, b, n + 1)
                        return
                    banks = acc[:, 2 * (n % 2):2 * (n % 2) + 2, :]
                    act.wait_ge(dn_ok[p].sem, dn_ok[p].ready(G))
                    if p == 2:
                        act.activation(split[:, 2 * n:2 * n + 2, 2 * C:3 * C], banks[:, :, 0:C], ACT.Copy).then_inc(hi_ok.sem, 1)
                        act.wait_ge(u_stored.sem, u_stored.free(G, 2))
                        act.activation(u_s[n % 2], banks[:, :, C:2 * C], ACT.Copy).then_inc(ut_ok.sem, 1)
                        return
                    H = heads(p)
                    D = C // H
                    for i in range(2):
                        to = V[p][:, 2 * n + i, :].rearrange("p (h f) -> p h f", h=H)[:, :, 0:D]
                        act.activation(to, banks[:, i, 0:C].rearrange("p (h f) -> p h f", h=H), ACT.Copy)
                    act.activation(sd[:, 2 * n:2 * n + 2, 0:2 * H], banks[:, :, C:C + 2 * H], ACT.Copy).then_inc(ev_ok[p].sem, 1)

                def spread(self, p, b):
                    H = heads(p)
                    act.wait_ge(gd[p], 4 * b + 3)
                    act.activation(vv[:, :, 0:H], dd[:, :, 0:H], ACT.Exp)
                    act.activation(gg[:, :, 0:H], dd[:, :, 0:H], ACT.Exp, scale=-(1 - SLOPE)).then_inc(ga[p], 1)

                def row_weights(self, p, b, q, h):
                    H, Q = heads(p), NQ * b + q
                    act.wait_ge(edge_ok[p].sem, edge_ok[p].ready(NT * H * Q - H + h))
                    act.wait_ge(sB_ok[p].sem, sB_ok[p].ready(H * Q + h))
                    act.activation(wB[:, h, :], psB[:, :], ACT.Exp, scale=1 - SLOPE).then_inc(wB_ok[p].sem, 1)

                def attend_start(self, p, b, q):
                    for h in range(heads(p)):
                        self.row_weights(p, b, q, h)

                def attend(self, p, b, q, J):
                    if J == NT - 1 and q < NQ - 1:
                        self.attend_start(p, b, q + 1)

                def attend_end(self, p, b, q):
                    if p == 1:
                        Q = NQ * b + q
                        for h in range(HEADS):
                            act.wait_ge(mm_ok[1].sem, mm_ok[1].ready(NT * HEADS * Q + NT * HEADS - HEADS + h))
                            act.wait_ge(y_ok.sem, y_ok.free(BLK * Q, 1))
                            act.activation(yT[h], acc[0:F + 1, h, :], ACT.Copy).then_inc(yT_ok.sem, 1)

                def result(self, b, q, k):
                    y, e = result_of(q, k)
                    n = BLK * (NQ * b + q) + k
                    act.wait_ge(y_ok.sem, y_ok.ready(n))
                    act.activation(e, y, ACT.Exp).then_inc(e_ok.sem, 1)

                def load_columns(self, b, q, k, m):
                    n = 4 * (4 * (NQ * b + q) + k) + m
                    act.wait_ge(c_cast.sem, c_cast.free(n, 4))
                    act.dma_start(cols[m], adj_r[:, bass.ds(NT * b + 4 * m, 4), bass.ds((4 * q + k) * P, P)]).then_inc(c_ld[m], 16)

                def mean(self, b, q, k, m, odd):
                    J = 4 * (NQ * b + q) + k
                    if k == 0 and m == 0 and not odd:
                        for first in range(2):
                            self.load_columns(b, q, 0, first)
                    act.wait_ge(c_ld[m], 16 * J + 16)
                    act.wait_ge(c_mm.sem, c_mm.free(4 * J + m, 4))
                    act.activation(cols_b[m], cols[m], ACT.Copy).then_inc(c_cast.sem, 1)
                    if k == 0 and m == 0 and not odd:
                        act.wait_ge(ev_ok[2].sem, ev_ok[2].ready(GROUPS * b + GROUPS - 1))
                        act.wait_ge(u_stored.sem, u_stored.ready(GROUPS * b + GROUPS - 1))
                        act.sem_inc(loads_begun, 1)
                        self.load_columns(b, q, 0, 2)
                    then = 4 * k + m + 3
                    if then < 16:
                        self.load_columns(b, q, then // 4, then % 4)
                    elif not odd:
                        self.load_columns(b, q + 1, 0, then % 4)

            program(act, Do())

        @block.tensor
        def _(pe):
            class Do(Part):
                def setup(self):
                    for c in (a_used, a_pack, cat_tr, o_done, tp_ok[1], tp_ok[2], tp_ok[3], dn_ok[1], dn_ok[2], dn_ok[3], mm_ok[1], mm_ok[3], c_mm):
                        pe.sem_inc(c.sem, c.credit)
                    pe.wait_ge(w_ld, 16 * N_LOADS)
                    for dk in range(2):
                        for ok in range(2):
                            ins = pe.transpose(psH[:, dk * C + ok * P:dk * C + ok * P + P], gath[:, 0, ok, dk * P:dk * P + P], ident)
                    ins.then_inc(w_tr, 1)
                    pe.wait_ge(w_cast, 2)
                    pe.wait_ge(w_done, 1)

                def slot_front(self, T, par, n, part):
                    def turn(half):
                        pe.wait_ge(a_copied.sem, a_copied.free(2 * T + half, 1))
                        for k in range(2):
                            pe.wait_ge(a_cast.sem, a_cast.ready(4 * T + 2 * half + k))
                            for j in range(4):
                                ins = pe.transpose(psT[:, 512 * k + P * j:512 * k + P * j + P], adj_b[:, k, P * j:P * j + P], ident_bf[:, :])
                            ins.then_inc(a_used.sem, 1)

                    def pack(half):
                        pe.wait_ge(a_evac.sem, a_evac.ready(2 * T + half))
                        if half == 0:
                            pe.wait_ge(a_key.sem, a_key.free(T, 1))
                        for j in range(8):
                            w = WPT * (8 * half + j)
                            ins = pe.matmul(words[:, w:w + WPT], adjT_b[:, P * j:P * j + P], pack_bf[:, :], start=True, stop=True)
                        ins.then_inc(a_pack.sem, 1)

                    if part in (0, 5):
                        turn((0, 5).index(part))
                    if part in (3, 7):
                        pack((3, 7).index(part))

                def slot_back(self, T, par, n, part, front):
                    if part == 7:
                        pe.wait_ge(cat_ld, 16 * T + 16)
                        pe.wait_ge(reduced.sem, reduced.ready(T))
                        pe.wait_ge(x1_done.sem, x1_done.free(T, 1))
                        for k in range(4):
                            ins = pe.transpose(psH[:, P * k:P * k + P], cat[:, P * k:P * k + P], ident)
                        ins.then_inc(cat_tr.sem, 1)
                    if part == 10:
                        pe.wait_ge(cat_ev.sem, cat_ev.ready(T))
                        pe.matmul(o_mm, one[0:1, :].to_broadcast([1, P]), bias[0:1, :], start=True, stop=False)
                        for k in range(4):
                            ins = pe.matmul(o_mm, catT[:, k, :], w0_s[:, k, :], start=False, stop=(k == 3))
                        ins.then_inc(o_done.sem, 1)

                def turn_h(self, p, b, n):
                    G = GROUPS * b + n
                    pe.wait_ge(h_ok[p].sem, h_ok[p].ready(G))
                    pe.wait_ge(hT_ok[p].sem, hT_ok[p].free(G, 1))
                    for i in range(2):
                        for c in range(2):
                            at = i * C + c * P
                            ins = pe.transpose(psB[:, at:at + P], hb[:, (2 * n + i) % BLK, c * P:c * P + P], ident)
                    ins.then_inc(tp_ok[p].sem, 1)

                def prep_start(self, p, b):
                    if p == 1:
                        pe.wait_ge(x3_ok.sem, x3_ok.free(NQ * b, 1))
                    self.turn_h(p, b, 0)

                def prep(self, p, b, n, part):
                    G = GROUPS * b + n
                    if part == 0:
                        if n < GROUPS - 1:
                            self.turn_h(p, b, n + 1)
                        return
                    pe.wait_ge(hT_ok[p].sem, hT_ok[p].ready(G))
                    pe.wait_ge(ev_ok[p].sem, ev_ok[p].free(G, 2))
                    w = {1: w1_s, 2: w2_s, 3: w3_s}[p]
                    width = w.shape[2]
                    for i in range(2):
                        bank = acc[:, 2 * (n % 2) + i, :]
                        for c in range(2):
                            ins = pe.matmul(bank[:, 0:width], hT[n % 2][:, i, c, :], w[:, c, :], start=(c == 0), stop=(c == 1 and p != 2),
                                            skip_group_check=True)
                        if p == 2:
                            ins = pe.matmul(bank[:, C:2 * C], one[32:33, :].to_broadcast([1, P]), bias[32:33, :], start=False, stop=True,
                                            skip_group_check=True)
                    ins.then_inc(dn_ok[p].sem, 1)

                def spread(self, p, b):
                    H = heads(p)
                    pe.wait_ge(gd[p], 4 * b + 1)
                    pe.transpose(psB[0:H, 0:P], dmx[:, 0:H], ident).then_inc(gp[p], 1)
                    pe.wait_ge(gd[p], 4 * b + 2)
                    pe.matmul(psB[:, P:P + H], one[0:H, :].to_broadcast([H, P]), ddiag[0:H, 0:H], start=True, stop=True).then_inc(gp[p], 1)

                def spread_row(self, p, b, q, h):
                    n = heads(p) * (NQ * b + q) + h
                    pe.wait_ge(wB_ok[p].sem, wB_ok[p].free(n, 1))
                    for k in range(BLK):
                        ins = pe.matmul(psB[:, P * k:P * k + P], sp_[:, BLK * q + k, h:h + 1].to_broadcast([P, P]), ident, start=True, stop=True)
                    ins.then_inc(sB_ok[p].sem, 1)

                def attend_start(self, p, b, q):
                    pe.wait_ge(gd[p], 4 * b + 3)
                    for h in range(heads(p)):
                        self.spread_row(p, b, q, h)

                def attend(self, p, b, q, J):
                    H, Q = heads(p), NQ * b + q
                    if J == 0:
                        pe.wait_ge(gd[p], 4 * b + 4)
                    if p == 3 and J == 0:
                        pe.wait_ge(x3_ok.sem, x3_ok.free(Q, 1))
                    ahead = J == NT - 1 and q < NQ - 1
                    if ahead and p == 1:
                        pe.wait_ge(y_ok.sem, y_ok.free(BLK * Q, 1))
                    for h in range(H):
                        n = H * J + h
                        if ahead:
                            self.spread_row(p, b, q + 1, h)
                        if p == 1 and J == 0:
                            pe.wait_ge(yT_ok.sem, yT_ok.free(H * Q + h, H))
                        pe.wait_ge(edge_ok[p].sem, edge_ok[p].ready(NT * H * Q + n))
                        if p == 1:
                            ins = pe.matmul(acc[0:F + 1, h, :], V[1][:, J, (F + 1) * h:(F + 1) * (h + 1)], edge[:, n % 4, :],
                                            start=(J == 0), stop=(J == NT - 1), skip_group_check=True)
                        else:
                            for k in range(BLK):
                                ins = pe.matmul(acc[:, k, 0:C + 1], edge[:, n % 4, P * k:P * k + P], V[3][:, J, :],
                                                start=(J == 0), stop=(J == NT - 1), skip_group_check=True)
                        ins.then_inc(mm_ok[p].sem, 1)

                def turn_back(self, b, q, k):
                    Q = NQ * b + q
                    if k == 0:
                        pe.wait_ge(yT_ok.sem, yT_ok.ready(HEADS * Q + HEADS - 1))
                        if q < NQ - 1:
                            pe.wait_ge(wB_ok[1].sem, wB_ok[1].ready(HEADS * Q + 2 * HEADS - 1))
                    pe.wait_ge(y_ok.sem, y_ok.free(BLK * Q + k, 1))
                    for h in range(HEADS):
                        ins = pe.transpose(psB[:, (F + 1) * h:(F + 1) * (h + 1)], yT[h][:, P * k:P * k + P], ident[0:F + 1, 0:F + 1])
                    ins.then_inc(back_ok.sem, 1)

                def mean(self, b, q, k, m, odd):
                    J = 4 * (NQ * b + q) + k
                    if m == 0:
                        if k == 0:
                            pe.wait_ge(ev_ok[2].sem, ev_ok[2].ready(GROUPS * b + GROUPS - 1))
                        pe.wait_ge(x2_ok.sem, x2_ok.free(J, 4))
                    pe.wait_ge(c_cast.sem, c_cast.ready(4 * J + m))
                    for i in range(4):
                        t = 4 * m + i
                        w = cols_b[m][:, i, :]
                        pe.matmul(acc[:, k, 0:C + 1], w, split[:, t, 2 * C:3 * C + 1], start=(t == 0), stop=False, skip_group_check=True)
                        pe.matmul(acc[:, k, 0:C], w, split[:, t, 0:C], start=False, stop=False, skip_group_check=True)
                        ins = pe.matmul(acc[:, k, 0:C], w, split[:, t, C:2 * C], start=False, stop=(t == NT - 1), skip_group_check=True)
                    ins.then_inc(c_mm.sem, 1)

            program(pe, Do())

        @block.vector
        def _(dve):
            class Steps:
                n = 0

                def of(self, ins):
                    ins.then_inc(chain, 1)
                    self.n += 1

                def wait(self):
                    dve.wait_ge(chain, self.n)

                def carry(self):
                    dve.sem_inc(chain, 1)
                    self.n += 1

                def end(self):
                    self.wait()
                    dve.sem_clear(chain)
                    self.n = 0

            steps = Steps()

            def deviation(mean, var, rstd, shift, tmp):
                steps.of(dve.tensor_scalar(var, var, EPS, None, ALU.add))
                steps.wait()
                steps.of(dve.tensor_scalar(tmp.bitcast(U32), var.bitcast(U32), 1, None, ALU.logical_shift_right))
                steps.wait()
                steps.of(dve.tensor_scalar(rstd.bitcast(U32), tmp.bitcast(U32), -1.0, float(0x5F3759DF), ALU.mult, ALU.add))
                for _ in range(3):
                    steps.wait()
                    steps.of(dve.scalar_tensor_tensor(tmp, rstd, -0.5, rstd, ALU.mult, ALU.mult))
                    steps.wait()
                    steps.of(dve.tensor_tensor(tmp, tmp, var, ALU.mult))
                    steps.wait()
                    steps.of(dve.scalar_tensor_tensor(rstd, tmp, 1.5, rstd, ALU.add, ALU.mult))
                steps.wait()
                return dve.scalar_tensor_tensor(shift, mean, -1.0, rstd, ALU.mult, ALU.mult)

            def block_stats(q):
                for k in range(BLK):
                    steps.of(dve.bn_stats(st[:, bass.ds(BLK * q + k, 1), :].rearrange("p t c -> p (t c)"),
                                          xr[:, bass.ds(BLK * q + k, 1), :].rearrange("p t c -> p (t c)")))

            def first_bits(values, r0, r1, rounds=4):
                for r in range(r0, r1):
                    steps.of(dve.max(top[:, 8 * r:8 * r + 8], values))
                    steps.wait()
                    if r < rounds - 1:
                        steps.of(dve.match_replace(values, top[:, 8 * r:8 * r + 8], values, 0.0))
                        steps.wait()

            class Do(Part):
                def setup(self):
                    for c in (a_key, reduced, x1_done, ev_ok[2], edge_ok[1], edge_ok[3], y_ok, x3_ok, x2_ok):
                        dve.sem_inc(c.sem, c.credit)
                    dve.memset(gath[:, 1, 0:NT, :], 0.0).then_inc(zero_set, 1)
                    dve.sem_inc(a_ln.sem, NT)
                    dve.wait_ge(w_ld, 16 * N_LOADS)
                    steps.of(dve.tensor_copy(bit_u[:, :], cst[:, C_BIT:C_BIT + WORD]))
                    steps.of(dve.tensor_scalar(bias[0:1, :], bias[0:1, :], -1.0, None, ALU.add))
                    scratch = cat[:, 0:C]
                    dve.wait_ge(w_ev, 1)
                    for w, k, at, a, H in [(w1_s, k, C, 2, HEADS) for k in range(2)] + [(w1_s, k, C + HEADS, 3, HEADS) for k in range(2)] \
                            + [(w3_s, k, C, 4, 1) for k in range(2)] + [(w3_s, k, C + 1, 5, 1) for k in range(2)]:
                        steps.of(dve.tensor_tensor(scratch, w[:, k, 0:C], gath[:, 0, a, :], ALU.mult))
                        steps.wait()
                        steps.of(dve.tensor_reduce(w[:, k, at:at + H], scratch.rearrange("p (h f) -> p h f", h=H), AX, ALU.add))
                        steps.wait()
                    steps.end()
                    dve.sem_inc(w_done, 1)
                    dve.wait_ge(w_done, 1)

                def first_h(self):
                    for g in range(NQ):
                        dve.wait_ge(x0_ld[g % 2], 16 * (g // 2) + 16)
                        for t in range(BLK * g, BLK * g + BLK):
                            steps.of(dve.bn_stats(st[:, t, :], xr[:, t, :]))
                    steps.wait()
                    for t in range(NT):
                        steps.of(dve.bn_aggr(mv[:, t, :], st[:, t, :]))
                    steps.wait()
                    deviation(mv[:, :, 0], mv[:, :, 1], rs[:, :], nm[:, :], tmp[:, :]).then_inc(ln0_ok, 1)
                    steps.end()

                def pre(self, u, n, part):
                    if part != 8:
                        return
                    for i in range(2):
                        dve.wait_ge(xa_ld[i], 16 * (n - NT // 2) + 16)
                        dve.wait_ge(a_relu.sem, a_relu.free(u + i, 2))
                        steps.of(dve.bn_stats(st_a[:, i, :], xa[:, i, :]))
                    steps.wait()
                    for i in range(2):
                        steps.of(dve.bn_aggr(mv_a[:, i, :], st_a[:, i, :]))
                    steps.wait()
                    deviation(mv_a[:, :, 0], mv_a[:, :, 1], rn_a[:, :, 0], rn_a[:, :, 1], tmp_a[:, :]).then_inc(a_ln.sem, 2)
                    steps.end()

                def slot_front(self, T, par, n, part):
                    if part == 12:
                        dve.wait_ge(a_pack.sem, a_pack.ready(2 * T + 1))
                        steps.of(dve.scalar_tensor_tensor(key[:, :], words, 0.0, cst[:, C_BASE:C_BASE + NW], ALU.is_gt, ALU.mult))
                        steps.wait()
                        dve.tensor_tensor(key[:, :], key[:, :], words, ALU.add).then_inc(a_key.sem, 1)
                        dve.wait_ge(a_key.sem, a_key.ready(T))
                        steps.carry()
                        first_bits(key[:, :], 0, 2)
                    if part == 13:
                        first_bits(key[:, :], 2, 4)
                    if part == 14:
                        steps.of(dve.tensor_copy(topu[:, :], top[:, 0:S]))
                        steps.wait()
                        steps.of(dve.tensor_scalar(hi8[:, :], topu[:, :], 8, 3, ALU.logical_shift_right, ALU.logical_shift_left))
                        steps.of(dve.tensor_tensor(bits[:, :, :], topu[:, :].unsqueeze(2).to_broadcast([P, S, WORD]),
                                                   bit_u[:, :].unsqueeze(1).to_broadcast([P, S, WORD]), ALU.bitwise_and))
                        steps.wait()
                        steps.of(dve.tensor_tensor(score[:, :, :], hi8[:, :].unsqueeze(2).to_broadcast([P, S, WORD]),
                                                   cst[:, C_R:C_R + WORD].unsqueeze(1).to_broadcast([P, S, WORD]), ALU.subtract))
                        steps.wait()
                        steps.of(dve.scalar_tensor_tensor(score[:, :, :], bits[:, :, :], 0.0, score[:, :, :], ALU.is_gt, ALU.mult))
                        steps.wait()
                        first_bits(key[:, 0:S * WORD], 0, 1)
                    if part == 15:
                        first_bits(key[:, 0:S * WORD], 1, 4)
                        dve.tensor_scalar(idx[:, par, :], top[:, 0:S], -1.0, cst[:, bass.ds(T + C_OFF, 1)], ALU.mult, ALU.add)\
                           .then_inc(idx_ready.sem, 1)
                        dve.wait_ge(idx_ready.sem, idx_ready.ready(T))
                        steps.carry()
                    if part in (12, 13, 14, 15):
                        steps.end()

                def slot_back(self, T, par, n, part, front):
                    if part == 0:
                        dve.wait_ge(gathered[par], 16 * S * n + 16 * S)
                        dve.wait_ge(cat_tr.sem, cat_tr.free(T, 1))
                    if part < 4:
                        c0, c1 = part * C // 4, (part + 1) * C // 4
                        ins = dve.tensor_reduce(cat[:, C + c0:C + c1], gath[:, par, :, c0:c1].rearrange("p s c -> p c s"), AX, ALU.max)
                        if part == 3:
                            ins.then_inc(reduced.sem, 1)
                    if part == 15:
                        dve.wait_ge(o_done.sem, o_done.ready(T))
                        dve.wait_ge(x1_ld, 16 * T + 16)
                        dve.scalar_tensor_tensor(x1[:, :], o_mm, -1.0, x1[:, :], ALU.max, ALU.add).then_inc(x1_done.sem, 1)

                def prep(self, p, b, n, part):
                    G = GROUPS * b + n
                    if p == 2 and part == 1:
                        here = slice(2 * n, 2 * n + 2)
                        hi, mid, low = split[:, here, 2 * C:3 * C], split[:, here, 0:C], split[:, here, C:2 * C]
                        rest = res[n % 2]
                        dve.wait_ge(hi_ok.sem, hi_ok.ready(G))
                        dve.wait_ge(ut_ok.sem, ut_ok.ready(G))
                        steps.of(dve.tensor_tensor(rest, acc[:, 2 * (n % 2):2 * (n % 2) + 2, 0:C], hi, ALU.subtract))
                        steps.wait()
                        steps.of(dve.tensor_copy(mid, rest))
                        steps.wait()
                        steps.of(dve.tensor_tensor(rest, rest, mid, ALU.subtract))
                        steps.wait()
                        dve.tensor_copy(low, rest).then_inc(ev_ok[2].sem, 1)
                        dve.wait_ge(ev_ok[2].sem, ev_ok[2].ready(G))
                        steps.carry()
                        steps.end()

                def norm(self, p, b, half):
                    t0, t1 = NT // 2 * half, NT // 2 * half + NT // 2
                    if p == 1:
                        for g in range(2 * half, 2 * half + 2):
                            dve.wait_ge(xr_ld[g % 2], 16 * (2 * b + half) + 32)
                            for t in range(BLK * g, BLK * g + BLK):
                                steps.of(dve.bn_stats(st[:, t, :], xr[:, t, :]))
                        steps.wait()
                    if p == 2 and half == 1:
                        steps.of(dve.memset(split[:, :, 3 * C:3 * C + 1], 1.0))
                    for t in range(t0, t1):
                        steps.of(dve.bn_aggr(mv[:, t, :], st[:, t, :]))
                    steps.wait()
                    deviation(mv[:, t0:t1, 0], mv[:, t0:t1, 1], rs[:, t0:t1], nm[:, t0:t1], tmp[:, t0:t1]).then_inc(ln_ok[p].sem, 1)
                    steps.end()

                def spread(self, p, b):
                    H = heads(p)
                    dve.wait_ge(ev_ok[p].sem, ev_ok[p].ready(GROUPS * b + GROUPS - 1))
                    dve.tensor_reduce(dmx[:, 0:H], sd[:, :, H:2 * H].rearrange("p t h -> p h t"), AX, ALU.max).then_inc(gd[p], 1)
                    dve.wait_ge(gp[p], 2 * b + 1)
                    steps.of(dve.tensor_reduce(dtop[0:H, :], psB[0:H, 0:P], AX, ALU.max))
                    steps.wait()
                    dve.tensor_scalar(ddiag[0:H, 0:H], cst[0:H, C_ID:C_ID + H], dtop[0:H, :], None, ALU.mult).then_inc(gd[p], 1)
                    dve.wait_ge(gp[p], 2 * b + 2)
                    D = psB[:, P:P + H].unsqueeze(1).to_broadcast([P, NT, H])
                    steps.of(dve.tensor_tensor(dd[:, :, 0:H], sd[:, :, H:2 * H], D, ALU.subtract))
                    steps.of(dve.tensor_tensor(sp_[:, :, 0:H], sd[:, :, 0:H], D, ALU.add))
                    steps.wait()
                    steps.of(dve.tensor_scalar(sp_[:, :, 0:H], sp_[:, :, 0:H], LIM, None, ALU.min))
                    dve.tensor_scalar(dd[:, :, 0:H], dd[:, :, 0:H], -LIM, None, ALU.max).then_inc(gd[p], 1)
                    dve.wait_ge(ga[p], b + 1)
                    W = C // H + 1
                    vals = V[p].rearrange("p t (h f) -> p t h f", h=H)
                    steps.of(dve.tensor_copy(vals[:, :, :, W - 1], vv[:, :, 0:H]))
                    steps.end()
                    dve.sem_inc(gd[p], 1)

                def attend(self, p, b, q, J):
                    H, Q = heads(p), NQ * b + q
                    if J == 0:
                        dve.wait_ge(a_copied.sem, a_copied.ready(2 * NT * b + 2 * NT - 1))
                        steps.carry()
                        steps.end()
                    if q == 0:
                        vals = V[p][:, J, :].rearrange("p (h f) -> p h f", h=H)
                        D = C // H
                        dve.tensor_tensor(vals[:, :, 0:D], vals[:, :, 0:D], vv[:, J, 0:H].unsqueeze(2).to_broadcast([P, H, D]), ALU.mult)
                    for h in range(H):
                        n = H * J + h
                        if J == 0:
                            dve.wait_ge(wB_ok[p].sem, wB_ok[p].ready(H * Q + h))
                        dve.wait_ge(mm_ok[p].sem, mm_ok[p].free(NT * H * Q + n, 4))
                        dve.scalar_tensor_tensor(
                            edge[:, n % 4, :], wB[:, h, :], gg[:, J, h:h + 1],
                            adjT[:, J, bass.ds(((b + (p - 1)) % 2) * N + 512 * q, 512)], ALU.max, ALU.mult).then_inc(edge_ok[p].sem, 1)

                def result(self, b, q, k):
                    y, e = result_of(q, k)
                    n = BLK * (NQ * b + q) + k
                    dve.wait_ge(back_ok.sem, back_ok.ready(n))
                    sums = psB[:, 0:HEADS * (F + 1)].rearrange("p (h f) -> p h f", h=HEADS)
                    steps.of(dve.reciprocal(den[:, k, :], sums[:, :, F]))
                    steps.wait()
                    dve.tensor_tensor(y.rearrange("p (h f) -> p h f", h=HEADS), sums[:, :, 0:F],
                                      den[:, k, :].unsqueeze(2).to_broadcast([P, HEADS, F]), ALU.mult).then_inc(y_ok.sem, 1)
                    steps.end()

                def add(self, b, q, k):
                    y, e = result_of(q, k)
                    t, n = BLK * q + k, BLK * (NQ * b + q) + k
                    dve.wait_ge(e_ok.sem, e_ok.ready(n))
                    steps.of(dve.scalar_tensor_tensor(e, e, 1.0, xr[:, t, :], ALU.min, ALU.add))
                    steps.wait()
                    steps.of(dve.scalar_tensor_tensor(xr[:, t, :], y, 0.0, e, ALU.max, ALU.add))
                    steps.wait()
                    steps.of(dve.bn_stats(st[:, t, :], xr[:, t, :]))
                    steps.end()

                def attend_end(self, p, b, q):
                    if p == 1:
                        return
                    Q = NQ * b + q
                    dve.wait_ge(mm_ok[3].sem, mm_ok[3].ready(NT * Q + NT - 1))
                    steps.of(dve.reciprocal(den[:, :, 0:1], acc[:, :, C:C + 1]))
                    steps.wait()
                    for k in range(BLK):
                        row = xr[:, bass.ds(BLK * q + k, 1), :].rearrange("p t c -> p (t c)")
                        ins = dve.scalar_tensor_tensor(row, acc[:, k, 0:C], den[:, k, 0:1], row, ALU.mult, ALU.add)
                    ins.then_inc(x3_ok.sem, 1)
                    steps.end()

                def mean(self, b, q, k, m, odd):
                    if m == 1 and k > 0:
                        self.finish(b, q, k - 1)
                    if m == 3 and k == BLK - 1:
                        self.finish(b, q, k)

                def finish(self, b, q, k):
                    J = 4 * (NQ * b + q) + k
                    if k == 0:
                        dve.wait_ge(u_ld, 16 * (NQ * b + q) + 16)
                    dve.wait_ge(c_mm.sem, c_mm.ready(4 * J + 3))
                    steps.of(dve.tensor_scalar(den[:, k, 0:1], acc[:, k, C:C + 1], 1.0, None, ALU.max))
                    steps.wait()
                    steps.of(dve.reciprocal(den[:, k, 1:2], den[:, k, 0:1]))
                    steps.wait()
                    y2 = edge_f[:, 4 * C:5 * C]
                    steps.of(dve.scalar_tensor_tensor(y2, acc[:, k, 0:C], den[:, k, 1:2], u2_s[:, k, :], ALU.mult, ALU.add))
                    steps.wait()
                    row = xr[:, bass.ds(BLK * q + k, 1), :].rearrange("p t c -> p (t c)")
                    dve.scalar_tensor_tensor(row, y2, 0.0, row, ALU.max, ALU.add).then_inc(x2_ok.sem, 1)
                    dve.wait_ge(x2_ok.sem, x2_ok.ready(J))
                    if k == BLK - 1:
                        block_stats(q)
                    else:
                        steps.carry()
                    steps.end()

            program(dve, Do())


N_LOADS = 11
_INS = ["x", "adj", "L0_gnn_W", "L0_gnn_b", "L1_gnn_W", "L1_gnn_a_src", "L1_gnn_a_dst", "L2_gnn_W_msg", "L2_gnn_W_upd",
        "L2_gnn_bias", "L3_gnn_W", "L3_gnn_a"]


def kernel(**inputs):
    import numpy as np
    import concourse.bacc as bacc
    from concourse.bass_utils import run_bass_kernel_spmd

    nc = bacc.Bacc("TRN2", target_bir_lowering=False, num_devices=1)
    arrays = {f"in_{n}": np.ascontiguousarray(inputs[n]) for n in _INS}
    arrays["in_const"] = constants()
    args = [nc.dram_tensor(n, a.shape, mybir.dt.from_np(a.dtype), kind="ExternalInput").ap() for n, a in arrays.items()]
    out = nc.dram_tensor("out_0", (B, N, C), F32, kind="ExternalOutput").ap()
    gnn_kernel(nc, *args, out)
    r = run_bass_kernel_spmd(nc, [arrays], core_ids=[0])
    return r.results[0]["out_0"]
```
